# Optimizing a Trainium2 kernel written in Bass

```python
import numpy as np
import jax
import jax.numpy as jnp

def _softmax(x, axis=-1):
    return jax.nn.softmax(x, axis=axis)

def _gelu(x):
    return jax.nn.gelu(x, approximate=True)

def _silu(x):
    return jax.nn.silu(x)

def _sigmoid(x):
    return jax.nn.sigmoid(x)

def _layernorm(x, axis=-1, eps=1e-05):
    m = jnp.mean(x, axis=axis, keepdims=True)
    v = jnp.var(x, axis=axis, keepdims=True)
    return (x - m) / jnp.sqrt(v + eps)

def _scatter_add(tgt, idx, src, axis=0):
    return tgt.at[idx].add(src)

def _segment_sum(src, seg, n):
    return jax.ops.segment_sum(src, seg, n)
kernel_name = 'mk_early_fusion_embed_d1_tok_img768_r4_04deea'

def setup_inputs(seed: int=0):
    np.random.seed(seed)
    _w = jnp.asarray

    def _rec_inputs():
        import jax
        import jax.numpy as jnp
        _rk = jax.random.key(seed)
        x = -7.10856e-05 + 0.999911 * jax.random.normal(jax.random.fold_in(_rk, 1), (2, 32, 128, 128), jnp.float32)
        x_txt = jax.random.randint(jax.random.fold_in(_rk, 51), (2, 32), 0, 30522, jnp.int32)
        return (x, x_txt)
    x, x_txt = _rec_inputs()

    def _L0_tok_setup():
        import jax, jax.numpy as jnp
        import numpy as np
        B, C, H, W = (8, 32, 128, 128)
        P = 8
        D = 128
        NH, DH = (8, 64)
        M = 512
        L = 2
        DOUT = 192
        INNER = NH * DH

        def _ln(x, g, b, eps=1e-05):
            mu = x.mean(-1, keepdims=True)
            xc = x - mu
            var = (xc * xc).mean(-1, keepdims=True)
            return xc * jax.lax.rsqrt(var + eps) * g + b

        def _forward(im, conv_w, conv_b, ln1_g, ln1_b, qkv_w, out_w, out_b, ln2_g, ln2_b, ff1_w, ff1_b, ff2_w, ff2_b, lnf_g, lnf_b, head_w, head_b):
            b, c, h, w = im.shape
            hp, wp = (h // P, w // P)
            patches = im.reshape(b, c, hp, P, wp, P)
            x = jnp.einsum('bchpwq,dcpq->bhwd', patches, conv_w)
            x = x.reshape(b, hp * wp, -1) + conv_b
            n = hp * wp
            scale = DH ** (-0.5)
            for i in range(ln1_g.shape[0]):
                y = _ln(x, ln1_g[i], ln1_b[i])
                qkv = y @ qkv_w[i]
                q, k, v = jnp.split(qkv, 3, axis=-1)
                to_heads = lambda t: t.reshape(b, n, NH, DH).transpose(0, 2, 1, 3)
                q, k, v = (to_heads(q), to_heads(k), to_heads(v))
                q = jax.nn.softmax(q, axis=-1) * scale
                k = jax.nn.softmax(k, axis=-2)
                ctx = jnp.einsum('bhnd,bhne->bhde', k, v)
                att = jnp.einsum('bhnd,bhde->bhne', q, ctx)
                att = att.transpose(0, 2, 1, 3).reshape(b, n, INNER)
                x = x + att @ out_w[i] + out_b[i]
                y = _ln(x, ln2_g[i], ln2_b[i])
                hdn = jax.nn.gelu(y @ ff1_w[i] + ff1_b[i], approximate=False)
                x = x + hdn @ ff2_w[i] + ff2_b[i]
            return _ln(x, lnf_g, lnf_b) @ head_w + head_b
        key = jax.random.key(seed)
        ks = iter(jax.random.split(key, 32))
        g = lambda shape, s=0.02: (jax.random.normal(next(ks), shape) * s).astype(jnp.float32)
        inp = {'im': jax.random.normal(next(ks), (B, C, H, W), dtype=jnp.float32), 'conv_w': g((D, C, P, P)), 'conv_b': jnp.zeros((D,), jnp.float32), 'ln1_g': jnp.ones((L, D), jnp.float32), 'ln1_b': jnp.zeros((L, D), jnp.float32), 'qkv_w': g((L, D, 3 * INNER)), 'out_w': g((L, INNER, D)), 'out_b': jnp.zeros((L, D), jnp.float32), 'ln2_g': jnp.ones((L, D), jnp.float32), 'ln2_b': jnp.zeros((L, D), jnp.float32), 'ff1_w': g((L, D, M)), 'ff1_b': jnp.zeros((L, M), jnp.float32), 'ff2_w': g((L, M, D)), 'ff2_b': jnp.zeros((L, D), jnp.float32), 'lnf_g': jnp.ones((D,), jnp.float32), 'lnf_b': jnp.zeros((D,), jnp.float32), 'head_w': g((D, DOUT)), 'head_b': jnp.zeros((DOUT,), jnp.float32)}
        return inp
    _L0_tok_all = _L0_tok_setup()
    _L0_tok_in = {k: v for k, v in _L0_tok_all.items() if k in ('conv_w', 'conv_b', 'ln1_g', 'ln1_b', 'qkv_w', 'out_w', 'out_b', 'ln2_g', 'ln2_b', 'ff1_w', 'ff1_b', 'ff2_w', 'ff2_b', 'lnf_g', 'lnf_b', 'head_w', 'head_b')}
    del _L0_tok_all

    def _L0_txt_setup():
        import jax, jax.numpy as jnp
        import numpy as np
        from jax import lax
        VOCAB = 30522
        MAX_POS = 128
        HIDDEN = 192
        LN_EPS = 1e-12

        def _forward(input_ids, word_emb, pos_emb, conv_w, ln_gamma, ln_beta):
            B, S = input_ids.shape
            we = word_emb[input_ids]
            pe = pos_emb[jnp.arange(S)][None, :, :]
            pe = jnp.broadcast_to(pe, we.shape)
            x = jnp.stack([we, pe], axis=1)
            y = lax.conv_general_dilated(x, conv_w, window_strides=(1, 1), padding=((1, 1), (1, 1)), dimension_numbers=('NCHW', 'OIHW', 'NCHW'))
            y = jax.nn.gelu(y[:, 0], approximate=False)
            mu = jnp.mean(y, axis=-1, keepdims=True)
            var = jnp.mean(jnp.square(y - mu), axis=-1, keepdims=True)
            out = (y - mu) * lax.rsqrt(var + LN_EPS) * ln_gamma + ln_beta
            return out
        key = jax.random.key(seed)
        k1, k2, k3, k4 = jax.random.split(key, 4)
        B, S, H = (64, 128, HIDDEN)
        input_ids = jax.random.randint(k1, (B, S), 0, VOCAB, dtype=jnp.int32)
        word_emb = jax.random.normal(k2, (VOCAB, H), dtype=jnp.float32) * 0.02
        word_emb = word_emb.at[0].set(0.0)
        pos_emb = jax.random.normal(k3, (MAX_POS, H), dtype=jnp.float32) * 0.02
        conv_w = jax.random.normal(k4, (1, 2, 3, 3), dtype=jnp.float32) * 0.1
        ln_gamma = jnp.ones((H,), dtype=jnp.float32)
        ln_beta = jnp.zeros((H,), dtype=jnp.float32)
        return {'input_ids': input_ids, 'word_emb': word_emb, 'pos_emb': pos_emb, 'conv_w': conv_w, 'ln_gamma': ln_gamma, 'ln_beta': ln_beta}
    _L0_txt_all = _L0_txt_setup()
    _L0_txt_in = {k: v for k, v in _L0_txt_all.items() if k in ('word_emb', 'pos_emb', 'conv_w', 'ln_gamma', 'ln_beta')}
    del _L0_txt_all

    def _L0_attn_setup():
        import jax, jax.numpy as jnp
        import numpy as np
        from jax import lax
        BATCH, L, D, N = (2, 1024, 192, 16)

        def _ssm_forward(x, A, W_B, b_B, W_C, b_C, W_D, b_D, p_Delta):
            Bproj = x @ W_B + b_B
            Cproj = x @ W_C + b_C
            delta = jax.nn.softplus(x @ W_D + b_D + p_Delta)
            dA = delta[..., None] * A
            A_bar = jnp.exp(dA)
            B_bar = (A_bar - A) / dA * delta[..., None] * Bproj[:, :, None, :]

            def step(h, inp):
                a, b, c, xl = inp
                h = a * h + b * xl[..., None]
                y = jnp.einsum('bn,bdn->bd', c, h)
                return (h, y)
            h0 = jnp.zeros((x.shape[0], D, N), dtype=x.dtype)
            xs = (jnp.moveaxis(A_bar, 1, 0), jnp.moveaxis(B_bar, 1, 0), jnp.moveaxis(Cproj, 1, 0), jnp.moveaxis(x, 1, 0))
            _, ys = lax.scan(step, h0, xs)
            return jnp.moveaxis(ys, 0, 1)
        key = jax.random.key(seed)
        ks = jax.random.split(key, 8)
        x = jax.random.normal(ks[0], (BATCH, L, D), dtype=jnp.float32)
        A = -jnp.tile((jnp.arange(N, dtype=jnp.float32) + 1.0)[None, :], (D, 1))
        s = 0.02
        W_B = jax.random.normal(ks[1], (D, N), dtype=jnp.float32) * s
        b_B = jnp.zeros((N,), dtype=jnp.float32)
        W_C = jax.random.normal(ks[2], (D, N), dtype=jnp.float32) * s
        b_C = jnp.zeros((N,), dtype=jnp.float32)
        W_D = jax.random.normal(ks[3], (D, 1), dtype=jnp.float32) * s
        b_D = jnp.zeros((1,), dtype=jnp.float32)
        p_Delta = jax.random.normal(ks[4], (D,), dtype=jnp.float32) * 0.1
        return {'x': x, 'A': A, 'W_B': W_B, 'b_B': b_B, 'W_C': W_C, 'b_C': b_C, 'W_D': W_D, 'b_D': b_D, 'p_Delta': p_Delta}
    _L0_attn_all = _L0_attn_setup()
    _L0_attn_in = {k: v for k, v in _L0_attn_all.items() if k in ('A', 'W_B', 'b_B', 'W_C', 'b_C', 'W_D', 'b_D', 'p_Delta')}
    del _L0_attn_all

    def _L0_ffn_setup():
        import jax, jax.numpy as jnp
        import numpy as np
        HIDDEN = 192
        INNER = 128
        EPS = 1e-05
        key = jax.random.key(seed)
        ks = jax.random.split(key, 6)
        B, S = (8, 1024)
        x = jax.random.normal(ks[0], (B, S, HIDDEN), dtype=jnp.float32)
        W1 = jax.random.normal(ks[1], (INNER, HIDDEN), dtype=jnp.float32) * 0.02
        b1 = jnp.zeros((INNER,), dtype=jnp.float32)
        W2 = jax.random.normal(ks[2], (HIDDEN, INNER), dtype=jnp.float32) * 0.02
        b2 = jnp.zeros((HIDDEN,), dtype=jnp.float32)
        bound = 1.0 / np.sqrt(HIDDEN)
        Wo = jax.random.uniform(ks[3], (HIDDEN, HIDDEN), minval=-bound, maxval=bound, dtype=jnp.float32)
        bo = jax.random.uniform(ks[4], (HIDDEN,), minval=-bound, maxval=bound, dtype=jnp.float32)
        gamma = jnp.ones((HIDDEN,), dtype=jnp.float32)
        beta = jnp.zeros((HIDDEN,), dtype=jnp.float32)
        return {'x': x, 'W1': W1, 'b1': b1, 'W2': W2, 'b2': b2, 'Wo': Wo, 'bo': bo, 'gamma': gamma, 'beta': beta}
    _L0_ffn_all = _L0_ffn_setup()
    _L0_ffn_in = {k: v for k, v in _L0_ffn_all.items() if k in ('W1', 'b1', 'W2', 'b2', 'Wo', 'bo', 'gamma', 'beta')}
    del _L0_ffn_all
    return {'x': x, 'x_txt': x_txt, 'L0_tok_conv_w': _L0_tok_in['conv_w'], 'L0_tok_conv_b': _L0_tok_in['conv_b'], 'L0_tok_ln1_g': _L0_tok_in['ln1_g'], 'L0_tok_ln1_b': _L0_tok_in['ln1_b'], 'L0_tok_qkv_w': _L0_tok_in['qkv_w'], 'L0_tok_out_w': _L0_tok_in['out_w'], 'L0_tok_out_b': _L0_tok_in['out_b'], 'L0_tok_ln2_g': _L0_tok_in['ln2_g'], 'L0_tok_ln2_b': _L0_tok_in['ln2_b'], 'L0_tok_ff1_w': _L0_tok_in['ff1_w'], 'L0_tok_ff1_b': _L0_tok_in['ff1_b'], 'L0_tok_ff2_w': _L0_tok_in['ff2_w'], 'L0_tok_ff2_b': _L0_tok_in['ff2_b'], 'L0_tok_lnf_g': _L0_tok_in['lnf_g'], 'L0_tok_lnf_b': _L0_tok_in['lnf_b'], 'L0_tok_head_w': _L0_tok_in['head_w'], 'L0_tok_head_b': _L0_tok_in['head_b'], 'L0_txt_word_emb': _L0_txt_in['word_emb'], 'L0_txt_pos_emb': _L0_txt_in['pos_emb'], 'L0_txt_conv_w': _L0_txt_in['conv_w'], 'L0_txt_ln_gamma': _L0_txt_in['ln_gamma'], 'L0_txt_ln_beta': _L0_txt_in['ln_beta'], 'L0_attn_A': _L0_attn_in['A'], 'L0_attn_W_B': _L0_attn_in['W_B'], 'L0_attn_b_B': _L0_attn_in['b_B'], 'L0_attn_W_C': _L0_attn_in['W_C'], 'L0_attn_b_C': _L0_attn_in['b_C'], 'L0_attn_W_D': _L0_attn_in['W_D'], 'L0_attn_b_D': _L0_attn_in['b_D'], 'L0_attn_p_Delta': _L0_attn_in['p_Delta'], 'L0_ffn_W1': _L0_ffn_in['W1'], 'L0_ffn_b1': _L0_ffn_in['b1'], 'L0_ffn_W2': _L0_ffn_in['W2'], 'L0_ffn_b2': _L0_ffn_in['b2'], 'L0_ffn_Wo': _L0_ffn_in['Wo'], 'L0_ffn_bo': _L0_ffn_in['bo'], 'L0_ffn_gamma': _L0_ffn_in['gamma'], 'L0_ffn_beta': _L0_ffn_in['beta']}

def reference(x, x_txt, L0_tok_conv_w, L0_tok_conv_b, L0_tok_ln1_g, L0_tok_ln1_b, L0_tok_qkv_w, L0_tok_out_w, L0_tok_out_b, L0_tok_ln2_g, L0_tok_ln2_b, L0_tok_ff1_w, L0_tok_ff1_b, L0_tok_ff2_w, L0_tok_ff2_b, L0_tok_lnf_g, L0_tok_lnf_b, L0_tok_head_w, L0_tok_head_b, L0_txt_word_emb, L0_txt_pos_emb, L0_txt_conv_w, L0_txt_ln_gamma, L0_txt_ln_beta, L0_attn_A, L0_attn_W_B, L0_attn_b_B, L0_attn_W_C, L0_attn_b_C, L0_attn_W_D, L0_attn_b_D, L0_attn_p_Delta, L0_ffn_W1, L0_ffn_b1, L0_ffn_W2, L0_ffn_b2, L0_ffn_Wo, L0_ffn_bo, L0_ffn_gamma, L0_ffn_beta):
    import jax
    import jax.numpy as jnp

    def _L0_tok_ref(im, conv_w, conv_b, ln1_g, ln1_b, qkv_w, out_w, out_b, ln2_g, ln2_b, ff1_w, ff1_b, ff2_w, ff2_b, lnf_g, lnf_b, head_w, head_b):
        import jax, jax.numpy as jnp
        import numpy as np
        B, C, H, W = (8, 32, 128, 128)
        P = 8
        D = 128
        NH, DH = (8, 64)
        M = 512
        L = 2
        DOUT = 192
        INNER = NH * DH

        def _ln(x, g, b, eps=1e-05):
            mu = x.mean(-1, keepdims=True)
            xc = x - mu
            var = (xc * xc).mean(-1, keepdims=True)
            return xc * jax.lax.rsqrt(var + eps) * g + b

        def _forward(im, conv_w, conv_b, ln1_g, ln1_b, qkv_w, out_w, out_b, ln2_g, ln2_b, ff1_w, ff1_b, ff2_w, ff2_b, lnf_g, lnf_b, head_w, head_b):
            b, c, h, w = im.shape
            hp, wp = (h // P, w // P)
            patches = im.reshape(b, c, hp, P, wp, P)
            x = jnp.einsum('bchpwq,dcpq->bhwd', patches, conv_w)
            x = x.reshape(b, hp * wp, -1) + conv_b
            n = hp * wp
            scale = DH ** (-0.5)
            for i in range(ln1_g.shape[0]):
                y = _ln(x, ln1_g[i], ln1_b[i])
                qkv = y @ qkv_w[i]
                q, k, v = jnp.split(qkv, 3, axis=-1)
                to_heads = lambda t: t.reshape(b, n, NH, DH).transpose(0, 2, 1, 3)
                q, k, v = (to_heads(q), to_heads(k), to_heads(v))
                q = jax.nn.softmax(q, axis=-1) * scale
                k = jax.nn.softmax(k, axis=-2)
                ctx = jnp.einsum('bhnd,bhne->bhde', k, v)
                att = jnp.einsum('bhnd,bhde->bhne', q, ctx)
                att = att.transpose(0, 2, 1, 3).reshape(b, n, INNER)
                x = x + att @ out_w[i] + out_b[i]
                y = _ln(x, ln2_g[i], ln2_b[i])
                hdn = jax.nn.gelu(y @ ff1_w[i] + ff1_b[i], approximate=False)
                x = x + hdn @ ff2_w[i] + ff2_b[i]
            return _ln(x, lnf_g, lnf_b) @ head_w + head_b
        return _forward(im, conv_w, conv_b, ln1_g, ln1_b, qkv_w, out_w, out_b, ln2_g, ln2_b, ff1_w, ff1_b, ff2_w, ff2_b, lnf_g, lnf_b, head_w, head_b)

    def _L0_txt_ref(input_ids, word_emb, pos_emb, conv_w, ln_gamma, ln_beta):
        import jax, jax.numpy as jnp
        import numpy as np
        from jax import lax
        VOCAB = 30522
        MAX_POS = 128
        HIDDEN = 192
        LN_EPS = 1e-12

        def _forward(input_ids, word_emb, pos_emb, conv_w, ln_gamma, ln_beta):
            B, S = input_ids.shape
            we = word_emb[input_ids]
            pe = pos_emb[jnp.arange(S)][None, :, :]
            pe = jnp.broadcast_to(pe, we.shape)
            x = jnp.stack([we, pe], axis=1)
            y = lax.conv_general_dilated(x, conv_w, window_strides=(1, 1), padding=((1, 1), (1, 1)), dimension_numbers=('NCHW', 'OIHW', 'NCHW'))
            y = jax.nn.gelu(y[:, 0], approximate=False)
            mu = jnp.mean(y, axis=-1, keepdims=True)
            var = jnp.mean(jnp.square(y - mu), axis=-1, keepdims=True)
            out = (y - mu) * lax.rsqrt(var + LN_EPS) * ln_gamma + ln_beta
            return out
        return _forward(input_ids, word_emb, pos_emb, conv_w, ln_gamma, ln_beta)

    def _L0_attn_ref(x, A, W_B, b_B, W_C, b_C, W_D, b_D, p_Delta):
        import jax, jax.numpy as jnp
        import numpy as np
        from jax import lax
        BATCH, L, D, N = (2, 1024, 192, 16)

        def _ssm_forward(x, A, W_B, b_B, W_C, b_C, W_D, b_D, p_Delta):
            Bproj = x @ W_B + b_B
            Cproj = x @ W_C + b_C
            delta = jax.nn.softplus(x @ W_D + b_D + p_Delta)
            dA = delta[..., None] * A
            A_bar = jnp.exp(dA)
            B_bar = (A_bar - A) / dA * delta[..., None] * Bproj[:, :, None, :]

            def step(h, inp):
                a, b, c, xl = inp
                h = a * h + b * xl[..., None]
                y = jnp.einsum('bn,bdn->bd', c, h)
                return (h, y)
            h0 = jnp.zeros((x.shape[0], D, N), dtype=x.dtype)
            xs = (jnp.moveaxis(A_bar, 1, 0), jnp.moveaxis(B_bar, 1, 0), jnp.moveaxis(Cproj, 1, 0), jnp.moveaxis(x, 1, 0))
            _, ys = lax.scan(step, h0, xs)
            return jnp.moveaxis(ys, 0, 1)
        return _ssm_forward(x, A, W_B, b_B, W_C, b_C, W_D, b_D, p_Delta)

    def _L0_ffn_ref(x, W1, b1, W2, b2, Wo, bo, gamma, beta):
        import jax, jax.numpy as jnp
        import numpy as np
        HIDDEN = 192
        INNER = 128
        EPS = 1e-05
        h = jax.nn.relu(jnp.einsum('bsd,id->bsi', x, W1) + b1)
        pred = jnp.einsum('bsi,di->bsd', h, W2) + b2
        out = jnp.einsum('bsd,ed->bse', pred, Wo) + bo
        mu = jnp.mean(out, axis=-1, keepdims=True)
        var = jnp.mean(jnp.square(out - mu), axis=-1, keepdims=True)
        out = (out - mu) * jax.lax.rsqrt(var + EPS) * gamma + beta
        return out
    h = _L0_tok_ref(x, L0_tok_conv_w, L0_tok_conv_b, L0_tok_ln1_g, L0_tok_ln1_b, L0_tok_qkv_w, L0_tok_out_w, L0_tok_out_b, L0_tok_ln2_g, L0_tok_ln2_b, L0_tok_ff1_w, L0_tok_ff1_b, L0_tok_ff2_w, L0_tok_ff2_b, L0_tok_lnf_g, L0_tok_lnf_b, L0_tok_head_w, L0_tok_head_b)
    h = jnp.concatenate([h, _L0_txt_ref(x_txt, L0_txt_word_emb, L0_txt_pos_emb, L0_txt_conv_w, L0_txt_ln_gamma, L0_txt_ln_beta)], axis=1)
    h = h + _L0_attn_ref(_layernorm(h, axis=-1), L0_attn_A, L0_attn_W_B, L0_attn_b_B, L0_attn_W_C, L0_attn_b_C, L0_attn_W_D, L0_attn_b_D, L0_attn_p_Delta)
    h = h + _L0_ffn_ref(_layernorm(h, axis=-1), L0_ffn_W1, L0_ffn_b1, L0_ffn_W2, L0_ffn_b2, L0_ffn_Wo, L0_ffn_bo, L0_ffn_gamma, L0_ffn_beta)
    return h

_drawn_inputs = setup_inputs


def setup_inputs(seed=0):
    import zlib

    import numpy as np

    out = dict(_drawn_inputs(seed))
    spreads = {'L0_tok_conv_b': (0.0, 0.1),
     'L0_tok_ln1_g': (1.0, 0.6),
     'L0_tok_ln1_b': (0.0, 0.8),
     'L0_tok_out_b': (0.0, 0.1),
     'L0_tok_ln2_g': (1.0, 0.6),
     'L0_tok_ln2_b': (0.0, 0.8),
     'L0_tok_ff1_b': (0.0, 0.1),
     'L0_tok_ff2_b': (0.0, 0.1),
     'L0_tok_lnf_g': (1.0, 0.2),
     'L0_tok_lnf_b': (0.0, 0.1),
     'L0_tok_head_b': (0.0, 0.1),
     'L0_txt_ln_gamma': (1.0, 0.2),
     'L0_txt_ln_beta': (0.0, 0.1),
     'L0_attn_b_B': (0.0, 0.1),
     'L0_attn_b_C': (0.0, 0.1),
     'L0_ffn_b1': (0.0, 0.1),
     'L0_ffn_b2': (0.0, 0.1),
     'L0_ffn_gamma': (1.0, 0.2),
     'L0_ffn_beta': (0.0, 0.1)}
    factors = {'L0_tok_qkv_w': 8.0, 'L0_tok_out_w': 8.0, 'L0_attn_p_Delta': 3.968}
    for name, (base, spread) in spreads.items():
        noise = np.random.default_rng([zlib.crc32(name.encode()), seed]).standard_normal(out[name].shape)
        drawn = base * np.exp(spread * noise) if base else spread * noise
        out[name] = jnp.asarray(drawn.astype(out[name].dtype))
    for name, factor in factors.items():
        out[name] = (out[name] * factor).astype(out[name].dtype)
    return out
```

```python
from contextlib import ExitStack

import numpy as np

import concourse.bass as bass
from concourse import mybir

F32 = mybir.dt.float32
BF16 = mybir.dt.bfloat16
I32 = mybir.dt.int32
ALU = mybir.AluOpType
ACT = mybir.ActivationFunctionType
AX = mybir.AxisListType.X

P = 128
NB = 2
D = 128
NT = 2
TOK = NT * P
KT = 16
KG = 4
LAYERS = 2
NH, DH = 8, 64
INNER = NH * DH
NJ = INNER // P
M = 512
NM = M // P
W = 192
W1 = W - P
S_TXT = 32
L = TOK + S_TXT
ROWS = [P, P, S_TXT]
N = 16
C0, C1 = N, N // 2
NC_ = C0 + C1
BANK = 512
FFI = 128

COL_LN = 0
COL_LNF = COL_LN + 4 * LAYERS
COL_FF1B = COL_LNF + 2
COL_BBC = COL_FF1B + NM * LAYERS
COL_B1 = COL_BBC + 1
COL_B2 = COL_B1 + 1
COL_PD = COL_B2 + 2
COL_BD = COL_PD + 2
COL_A = COL_BD + 1
COL_CW = COL_A + NC_
NCOLS = COL_CW + 18
ROW_CONVB = 0
ROW_OUTB = ROW_CONVB + D
ROW_FF2B = ROW_OUTB + LAYERS * D
ROW_HEADB = ROW_FF2B + LAYERS * D
ROW_BO = ROW_HEADB + W
ROW_FG = ROW_BO + W
ROW_FB = ROW_FG + W
ROW_TG = ROW_FB + W
ROW_TB = ROW_TG + W
NROWS = ROW_TB + W
MI_HEAD = 0
MI_BC = MI_HEAD + W
MI_WD = MI_BC + 2 * 2 * N
MI_W1 = MI_WD + 2 * P
MI_W2 = MI_W1 + 2 * FFI
MI_WO = MI_W2 + W
MI_FOLD = MI_WO + 2 * W
NMISC = MI_FOLD + W1
TC_SHIFT = 0
NTC = 3 * 2 * S_TXT

EPS = 1e-5
EPS_TXT = 1e-12


def build(nc, ids, patches, convw, qkvw, outw, ff1w, ff2w, cols_d, rows_d, misc_d, ident_d, tconst_d,
          sel_d, word_emb, pos_emb, out):
    ctx = ExitStack()
    with ctx:
        def sb(name, shape, dt=F32):
            return ctx.enter_context(nc.sbuf_tensor(name, shape, dt))

        def sem(name):
            return ctx.enter_context(nc.semaphore(name))

        def per_batch(make, name):
            return [make(f"{name}_{b}") for b in range(NB)]

        patch_sb = [sb(f"patch_{b}", [P, KT, TOK]) for b in range(NB)]
        convw_sb = sb("convw", [P, KT, D])
        qkv_sb = sb("qkvw", [P, LAYERS, 3 * INNER])
        outw_sb = sb("outw", [P, LAYERS, NJ, D])
        ff1_sb = sb("ff1w", [P, LAYERS, M])
        ff2_sb = sb("ff2w", [P, LAYERS, NM, D])
        cols = sb("cols", [P, NCOLS])
        rows = sb("rows", [P, NROWS])
        misc = sb("misc", [P, NMISC])
        ident = sb("ident", [P, P])
        tconst = sb("tconst", [2 * S_TXT, NTC])
        sel = sb("sel", [3 * 2 * N, 2 * C0 + 2 * C1, P], BF16)
        ids_sb = sb("ids", [2 * S_TXT, 1], I32)
        neghalf = sb("neghalf", [P, 4])
        inv_a = sb("inv_a", [P, NC_])
        pdelta = sb("pdelta", [P, 2])
        we = sb("word_rows", [2 * S_TXT, W + 2])
        pe_rows = sb("pos_rows", [2 * S_TXT, W + 2])
        band = sb("band", [2 * S_TXT, 6, 2 * S_TXT])
        band_t = sb("band_term", [2 * S_TXT, 6, 2 * S_TXT])
        txt = sb("txt", [S_TXT, NB, W])
        x = per_batch(lambda n: sb(n, [P, NT, D]), "x")
        xb = per_batch(lambda n: sb(n, [P, NT, D]), "x_plus_bias")
        xn = per_batch(lambda n: sb(n, [P, NT, D]), "x_normed")
        yt = per_batch(lambda n: sb(n, [P, TOK]), "y_t")
        stats = per_batch(lambda n: sb(n, [P, 3, 6]), "stats")
        mv = per_batch(lambda n: sb(n, [P, 3, 2]), "mean_var")
        ve = per_batch(lambda n: sb(n, [P, 3]), "var_eps")
        rstd = per_batch(lambda n: sb(n, [P, 3]), "rstd")
        kmax = per_batch(lambda n: sb(n, [P, NJ]), "neg_kmax")
        ksum = per_batch(lambda n: sb(n, [P, NJ]), "ksum")
        krec = per_batch(lambda n: sb(n, [P, NJ]), "krec")
        ekt = per_batch(lambda n: sb(n, [P, NJ, TOK]), "exp_k_t")
        kn = per_batch(lambda n: sb(n, [P, NT, INNER]), "exp_k")
        v = per_batch(lambda n: sb(n, [P, NT, INNER]), "v")
        qmax = per_batch(lambda n: sb(n, [P, NT * NH]), "qmax")
        qrec = per_batch(lambda n: sb(n, [P, NT * NH]), "qrec")
        q = per_batch(lambda n: sb(n, [P, NT * NH, DH]), "q")
        qt = per_batch(lambda n: sb(n, [P, NJ, TOK]), "q_t")
        ctxt = per_batch(lambda n: sb(n, [P, NJ, P]), "ctx_t")
        cw = per_batch(lambda n: sb(n, [P, NJ, D]), "ctx_outw")
        hid = ekt
        h = per_batch(lambda n: sb(n, [P, 3, W]), "h")
        hn = per_batch(lambda n: sb(n, [P, 3, 2 * P]), "h_normed")
        ht = per_batch(lambda n: sb(n, [P, 2, L]), "h_t")
        bc = per_batch(lambda n: sb(n, [2 * N, L]), "bc")
        bcr = per_batch(lambda n: sb(n, [2 * N, L]), "bc_rest")
        bc3 = per_batch(lambda n: sb(n, [3 * 2 * N, L], BF16), "bc_parts")
        z = per_batch(lambda n: sb(n, [P, 2, L]), "z")
        ez = per_batch(lambda n: sb(n, [P, 2, L]), "exp_z")
        delta = per_batch(lambda n: sb(n, [P, 2, L]), "delta")
        ys = ez
        fhid = per_batch(lambda n: sb(n, [P, L]), "ffn_hidden")
        fpred = z
        o = per_batch(lambda n: sb(n, [P, 3, W]), "o")
        RA, RM, RU, RB, RH = 8, 4, 4, 4, 4
        flat = [patch_sb[b][:].rearrange("p k n -> p (k n)") for b in range(NB)]

        def ring(b, first, n):
            return flat[b][:, first * L:(first + n) * L].rearrange("p (r n) -> p r n", r=n)

        abar, m = ring(0, 0, RA), ring(0, RA, RM)
        u, binc, hs = ring(1, 0, RU), ring(1, RU, RB), ring(1, RU + RB, RH)

        pa = [ctx.enter_context(nc.psum_tensor(f"pa_{b}", [P, 2 * BANK], F32)) for b in range(NB)]
        pb = [ctx.enter_context(nc.psum_tensor(f"pb_{b}", [P, 2 * BANK], F32)) for b in range(NB)]

        s_ids = sem("ids_loaded")
        s_patch = [[sem(f"patch_loaded_{b}_{g}") for g in range(KT // KG)] for b in range(NB)]
        s_convw = [sem(f"convw_loaded_{g}") for g in range(KT // KG)]
        s_cols, s_rows, s_misc, s_ident = sem("cols_loaded"), sem("rows_loaded"), sem("misc_loaded"), sem("ident_loaded")
        s_tconst, s_pos, s_word, s_sel = sem("tconst_loaded"), sem("pos_loaded"), sem("words_gathered"), sem("sel_loaded")
        s_qkv, s_outw, s_ff1, s_ff2 = sem("qkvw_loaded"), sem("outw_loaded"), sem("ff1w_loaded"), sem("ff2w_loaded")
        s_out = sem("out_written")
        s_init, s_fill, s_edges = sem("dve_fills_done"), sem("pool_fills_done"), sem("edges_zeroed")
        s_band, s_txtconv, s_txtgelu = sem("band_ready"), sem("txt_conv_done"), sem("txt_gelu_done")
        s_txtvar, s_txtrstd = sem("txt_var_ready"), sem("txt_rstd_ready")
        dve_step = sem("dve_step")
        pool_step = sem("pool_step")
        act_step = sem("act_step")
        conv_done = per_batch(sem, "conv_done")
        x_ready = per_batch(sem, "x_ready")
        xb_ready = per_batch(sem, "x_plus_bias_ready")
        var_ready = per_batch(sem, "var_ready")
        rstd_ready = per_batch(sem, "rstd_ready")
        xn_ready = per_batch(sem, "normed_ready")
        tr_done = per_batch(sem, "normed_transposed")
        yt_ready = per_batch(sem, "normed_t_ready")
        kt_done = per_batch(sem, "k_done")
        q_done = per_batch(sem, "q_done")
        v_done = per_batch(sem, "v_done")
        kmax_ready = per_batch(sem, "kmax_ready")
        ek_ready = per_batch(sem, "exp_k_ready")
        qsub_ready = per_batch(sem, "q_shifted")
        eq_ready = per_batch(sem, "exp_q_ready")
        qn_ready = per_batch(sem, "q_normed")
        v_ready = per_batch(sem, "v_copied")
        kn_done = per_batch(sem, "exp_k_transposed")
        kn_ready = per_batch(sem, "exp_k_copied")
        qt_done = per_batch(sem, "q_transposed")
        qt_ready = per_batch(sem, "q_t_copied")
        ctx_done = per_batch(sem, "ctx_done")
        ctx_ready = per_batch(sem, "ctx_copied")
        cw_done = per_batch(sem, "ctx_outw_done")
        cw_ready = per_batch(sem, "ctx_outw_copied")
        att_done = per_batch(sem, "att_done")
        ff1_done = per_batch(sem, "ff1_done")
        gelu_done = per_batch(sem, "gelu_done")
        ff2_done = per_batch(sem, "ff2_done")
        head_done = per_batch(sem, "head_done")
        bcd_done = per_batch(sem, "bc_delta_products_done")
        bc_ready = per_batch(sem, "bc_copied")
        z_ready = per_batch(sem, "z_ready")
        lnz_ready = per_batch(sem, "ln_exp_ready")
        bc3_ready = per_batch(sem, "bc_parts_ready")
        delta_ready = per_batch(sem, "delta_ready")
        b_spread = sem("b_spread")
        c_spread = sem("c_spread")
        abar_ready = sem("a_bar_ready")
        u_ready, binc_ready, hs_ready, m_ready = sem("u_ready"), sem("b_inc_ready"), sem("h_scan_ready"), sem("c_times_h_ready")
        m_summed = sem("c_times_h_summed")
        ys_ready = per_batch(sem, "y_scan_copied")
        yback_done = per_batch(sem, "y_scan_transposed")
        fhid_done = per_batch(sem, "ffn_hidden_done")
        fhid_ready = per_batch(sem, "ffn_hidden_ready")
        fpred_done = per_batch(sem, "ffn_pred_done")
        fpred_ready = per_batch(sem, "ffn_pred_ready")
        fout_done = per_batch(sem, "ffn_out_done")
        o_ready = per_batch(sem, "o_ready")

        block = ctx.enter_context(nc.Block())

        LNF, LN_SCAN, LN_FFN, LN_OUT = 2 * LAYERS, 2 * LAYERS + 1, 2 * LAYERS + 2, 2 * LAYERS + 3

        def col(c, n=1, r=P):
            return cols[0:r, c:c + n]

        def parts(c):
            return P if c == 0 else W1

        STAGES = [("conv", b, 0) for b in range(NB)]
        for l in range(LAYERS):
            for stage in ("att_norm", "att_in", "att_mid", "att_out", "ff_norm", "ff"):
                STAGES += [(stage, b, l) for b in range(NB)]
        STAGES += [("head", b, 0) for b in range(NB)]
        for b in range(NB):
            STAGES += [("scan_in", b, 0), ("scan", b, 0), ("scan_out", b, 0), ("ffn", b, 0)]

        @block.sync
        def _(sp):
            sp.dma_start(ids_sb[:], ids).then_inc(s_ids, 16)
            for g in range(KT // KG):
                k = slice(g * KG, (g + 1) * KG)
                sp.dma_start(convw_sb[:, k, :], convw[:, k, :]).then_inc(s_convw[g], 16)
                sp.dma_start(patch_sb[0][:, k, :], patches[0, :, k, :]).then_inc(s_patch[0][g], 16)
            sp.dma_start(ident[:], ident_d).then_inc(s_ident, 16)
            sp.dma_start(cols[:], cols_d).then_inc(s_cols, 16)
            sp.dma_start(rows[:], rows_d.partition_broadcast(P)).then_inc(s_rows, 16)
            for g in range(KT // KG):
                k = slice(g * KG, (g + 1) * KG)
                sp.dma_start(patch_sb[1][:, k, :], patches[1, :, k, :]).then_inc(s_patch[1][g], 16)
            sp.dma_start(qkv_sb[:], qkvw).then_inc(s_qkv, 16)
            sp.dma_start(outw_sb[:], outw).then_inc(s_outw, 16)
            sp.dma_start(ff1_sb[:], ff1w).then_inc(s_ff1, 16)
            sp.dma_start(ff2_sb[:], ff2w).then_inc(s_ff2, 16)
            sp.dma_start(misc[:], misc_d).then_inc(s_misc, 16)
            sp.dma_start(sel[:], sel_d).then_inc(s_sel, 16)
            for b in range(NB):
                sp.wait_ge(o_ready[b], 1)
                sp.dma_start(out[b, 0:TOK, :].rearrange("(t p) w -> p t w", p=P), o[b][:, 0:NT, :]).then_inc(s_out, 16)
                sp.dma_start(out[b, TOK:L, :], o[b][0:S_TXT, NT, :]).then_inc(s_out, 16)
            sp.wait_ge(s_out, 2 * NB * 16)

        @block.gpsimd
        def _(pool):
            nc.gpsimd.memset(we[:, 0:1], 0.0)
            nc.gpsimd.memset(we[:, W + 1:W + 2], 0.0)
            nc.gpsimd.memset(pe_rows[:, 0:1], 0.0)
            nc.gpsimd.memset(pe_rows[:, W + 1:W + 2], 0.0).then_inc(s_edges, 1)
            pool.dma_start(tconst[:], tconst_d).then_inc(s_tconst, 16)
            for b in range(NB):
                pool.dma_start(pe_rows[b * S_TXT:(b + 1) * S_TXT, 1:W + 1], pos_emb[0:S_TXT, :]).then_inc(s_pos, 16)
            pool.wait_ge(s_ids, 16)
            pool.indirect_dma_start(out=we[:, 1:W + 1], out_offset=None, in_=word_emb,
                                    in_offset=bass.IndirectOffsetOnAxis(ap=ids_sb[:, 0:1], axis=0)).then_inc(s_word, 16)
            nc.gpsimd.memset(neghalf[:], -0.5).then_inc(s_fill, 1)
            pool.wait_ge(s_fill, 1)

            def inverse_root(b, i, tiles):
                pool.wait_ge(var_ready[b], i + 1)
                nc.gpsimd.tensor_tensor(rstd[b][:, 0:tiles], ve[b][:, 0:tiles], neghalf[:, 0:tiles],
                                        ALU.pow).then_inc(rstd_ready[b], 1)

            def add_bias(b, k, row):
                pool.wait_ge(x_ready[b], k)
                nc.gpsimd.tensor_tensor(xb[b][:], x[b][:],
                                        rows[:, row:row + D].unsqueeze(1).to_broadcast([P, NT, D]),
                                        ALU.add).then_inc(xb_ready[b], 1)

            pool.wait_ge(s_txtvar, 1)
            nc.gpsimd.tensor_tensor(rstd[0][0:S_TXT, 0:NB], ve[0][0:S_TXT, 0:NB], neghalf[0:S_TXT, 0:NB],
                                    ALU.pow).then_inc(s_txtrstd, 1)
            pool.wait_ge(s_rows, 16)
            for stage, b, l in STAGES:
                if stage == "att_norm":
                    inverse_root(b, 2 * l, NT)
                    add_bias(b, 2 * l + 1, ROW_OUTB + l * D)
                elif stage == "ff_norm":
                    inverse_root(b, 2 * l + 1, NT)
                    add_bias(b, 2 * l + 2, ROW_FF2B + l * D)
                elif stage == "head":
                    inverse_root(b, LNF, NT)
                elif stage == "scan_in":
                    inverse_root(b, LN_SCAN, 3)
                elif stage == "ffn":
                    inverse_root(b, LN_FFN, 3)
                    inverse_root(b, LN_OUT, 3)

        @block.vector
        def _(dve):
            steps = [0]

            def link(ins):
                steps[0] += 1
                ins.then_inc(dve_step, 1)
                dve.wait_ge(dve_step, steps[0])

            def norm_stats(b, i, src, width, tiles, eps):
                for t in range(tiles):
                    last = nc.vector.bn_stats(stats[b][0:ROWS[t], t, :], src[0:ROWS[t], t, 0:width])
                link(last)
                for t in range(tiles):
                    last = nc.vector.bn_aggr(mv[b][0:ROWS[t], t, :], stats[b][0:ROWS[t], t, :])
                link(last)
                nc.vector.tensor_scalar(ve[b][:, 0:tiles], mv[b][:, 0:tiles, 1], eps, None,
                                        ALU.add).then_inc(var_ready[b], 1)

            def normalise(b, i, dst, src, width, tiles):
                dve.wait_ge(rstd_ready[b], i + 1)
                for t in range(tiles):
                    r = ROWS[t]
                    last = nc.vector.tensor_scalar(dst[0:r, t, 0:width], src[0:r, t, 0:width], mv[b][0:r, t, 0:1],
                                                   rstd[b][0:r, t:t + 1], ALU.subtract, ALU.mult)
                return last

            for b in range(NB):
                nc.vector.memset(ctxt[b][:], 0.0)
                last = nc.vector.memset(mv[b][:], 1.0)
            link(last)
            dve.wait_ge(s_cols, 16)
            dve.wait_ge(s_tconst, 16)
            for i in range(3):
                shift = tconst[:, i * 2 * S_TXT:(i + 1) * 2 * S_TXT].unsqueeze(1).to_broadcast([2 * S_TXT, 6, 2 * S_TXT])
                taps = col(COL_CW + 6 * i, 6, 2 * S_TXT).unsqueeze(2).to_broadcast([2 * S_TXT, 6, 2 * S_TXT])
                link(nc.vector.tensor_tensor((band if i == 0 else band_t)[:], shift, taps, ALU.mult))
                if i:
                    ins = nc.vector.tensor_tensor(band[:], band[:], band_t[:], ALU.add)
                    if i == 1:
                        link(ins)
                    else:
                        ins.then_inc(s_band, 1)
            nc.vector.reciprocal(inv_a[:], col(COL_A, NC_))
            nc.vector.tensor_tensor(pdelta[:], col(COL_PD, 2), col(COL_BD).to_broadcast([P, 2]), ALU.add)
            dve.wait_ge(s_txtgelu, 1)
            for b in range(NB):
                last = nc.vector.bn_stats(stats[0][0:S_TXT, b, :], txt[:, b, :])
            link(last)
            for b in range(NB):
                last = nc.vector.bn_aggr(mv[0][0:S_TXT, b, :], stats[0][0:S_TXT, b, :])
            link(last)
            nc.vector.tensor_scalar(ve[0][0:S_TXT, 0:NB], mv[0][0:S_TXT, 0:NB, 1], EPS_TXT, None,
                                    ALU.add).then_inc(s_txtvar, 1)
            dve.wait_ge(s_txtrstd, 1)
            for b in range(NB):
                last = nc.vector.tensor_scalar(txt[:, b, :], txt[:, b, :], mv[0][0:S_TXT, b, 0:1],
                                               rstd[0][0:S_TXT, b:b + 1], ALU.subtract, ALU.mult)
            link(last)
            dve.wait_ge(s_rows, 16)
            gains = rows[0:S_TXT, ROW_TG:ROW_TG + W].unsqueeze(1).to_broadcast([S_TXT, NB, W])
            link(nc.vector.tensor_tensor(txt[:], txt[:], gains, ALU.mult))
            for b in range(NB):
                nc.vector.tensor_tensor(h[b][0:S_TXT, NT, :], txt[:, b, :], rows[0:S_TXT, ROW_TB:ROW_TB + W], ALU.add)

            def scan_chunks(b):
                c0 = b * NC_
                dve.wait_ge(delta_ready[b], 1)

                def make_u(c):
                    g = c0 + c
                    dve.wait_ge(b_spread, g + 1)
                    if g >= RU:
                        dve.wait_ge(binc_ready, g - RU + 1)
                    nc.vector.tensor_tensor(u[:, g % RU, :], pb[b][:, 0:L], ht[b][:, 0 if c < C0 else 1, :],
                                            ALU.mult).then_inc(u_ready, 1)

                def make_b(c):
                    g = c0 + c
                    dve.wait_ge(u_ready, g + 1)
                    dve.wait_ge(abar_ready, g + 1)
                    if g >= RB:
                        dve.wait_ge(hs_ready, g - RB + 1)
                    nc.vector.scalar_tensor_tensor(binc[:, g % RB, :], abar[:, g % RA, :], col(COL_A + c),
                                                   u[:, g % RU, :], ALU.subtract, ALU.mult).then_inc(binc_ready, 1)

                def make_h(c):
                    g = c0 + c
                    dve.wait_ge(binc_ready, g + 1)
                    if g >= RH:
                        dve.wait_ge(m_ready, g - RH + 1)
                    nc.vector.tensor_tensor_scan(hs[:, g % RH, :], abar[:, g % RA, :], binc[:, g % RB, :], 0.0,
                                                 ALU.mult, ALU.add).then_inc(hs_ready, 1)

                def make_m(c):
                    g = c0 + c
                    dve.wait_ge(hs_ready, g + 1)
                    dve.wait_ge(c_spread, g + 1)
                    if g >= RM:
                        dve.wait_ge(m_summed, g - RM + 1)
                    nc.vector.scalar_tensor_tensor(m[:, g % RM, :], hs[:, g % RH, :], inv_a[:, c:c + 1],
                                                   pb[b][:, BANK:BANK + L], ALU.mult, ALU.mult).then_inc(m_ready, 1)

                for c in range(NC_ + 3):
                    if c >= 3:
                        make_m(c - 3)
                    if 2 <= c < NC_ + 2:
                        make_h(c - 2)
                    if 1 <= c < NC_ + 1:
                        make_b(c - 1)
                    if c < NC_:
                        make_u(c)

            for stage, b, l in STAGES:
                if stage == "conv":
                    dve.wait_ge(conv_done[b], 1)
                    nc.vector.tensor_tensor(x[b][:], pa[b][:].rearrange("p (t w) -> p t w", t=NT)[:, :, 0:D],
                                            rows[:, ROW_CONVB:ROW_CONVB + D].unsqueeze(1).to_broadcast([P, NT, D]),
                                            ALU.add).then_inc(x_ready[b], 1)
                elif stage in ("att_norm", "ff_norm"):
                    i = 2 * l + (stage == "ff_norm")
                    dve.wait_ge(x_ready[b], i + 1)
                    norm_stats(b, i, x[b], D, NT, EPS)
                    normalise(b, i, xn[b], x[b], D, NT).then_inc(xn_ready[b], 1)
                elif stage == "att_in":
                    dve.wait_ge(kt_done[b], l + 1)
                    nc.vector.tensor_reduce(kmax[b][:], pb[b][:].rearrange("p (j n) -> p j n", j=NJ), AX, ALU.max,
                                            negate=True).then_inc(kmax_ready[b], 1)
                    dve.wait_ge(q_done[b], l + 1)
                    link(nc.vector.tensor_reduce(qmax[b][:], pa[b][:].rearrange("p (h d) -> p h d", d=DH), AX, ALU.max))
                    nc.vector.tensor_tensor(q[b][:], pa[b][:].rearrange("p (h d) -> p h d", d=DH),
                                            qmax[b][:].unsqueeze(2).to_broadcast([P, NT * NH, DH]),
                                            ALU.subtract).then_inc(qsub_ready[b], 1)
                elif stage == "att_mid":
                    dve.wait_ge(eq_ready[b], l + 1)
                    link(nc.vector.tensor_reduce(qmax[b][:], q[b][:], AX, ALU.add))
                    link(nc.vector.reciprocal(qrec[b][:], qmax[b][:]))
                    nc.vector.tensor_tensor(q[b][:], q[b][:], qrec[b][:].unsqueeze(2).to_broadcast([P, NT * NH, DH]),
                                            ALU.mult).then_inc(qn_ready[b], 1)
                    dve.wait_ge(ek_ready[b], l + 1)
                    link(nc.vector.reciprocal(krec[b][:], ksum[b][:]))
                    nc.vector.tensor_scalar(krec[b][:], krec[b][:], DH ** -0.5, None, ALU.mult)
                elif stage == "att_out":
                    dve.wait_ge(ctx_done[b], l + 1)
                    for e in range(2):
                        r = slice(e * DH, (e + 1) * DH)
                        last = nc.vector.tensor_copy(ctxt[b][r, :, r],
                                                     pa[b][r, 0:BANK].rearrange("p (j d) -> p j d", j=NJ)[:, :, r])
                    last.then_inc(ctx_ready[b], 1)
                    dve.wait_ge(cw_done[b], l + 1)
                    nc.vector.tensor_tensor(cw[b][:], pa[b][:, BANK:2 * BANK].rearrange("p (j d) -> p j d", j=NJ),
                                            krec[b][:].unsqueeze(2).to_broadcast([P, NJ, D]),
                                            ALU.mult).then_inc(cw_ready[b], 1)
                    dve.wait_ge(att_done[b], l + 1)
                    dve.wait_ge(xb_ready[b], 2 * l + 1)
                    nc.vector.tensor_tensor(x[b][:], pb[b][:, 0:NT * D].rearrange("p (t d) -> p t d", t=NT), xb[b][:],
                                            ALU.add).then_inc(x_ready[b], 1)
                elif stage == "ff":
                    dve.wait_ge(ff2_done[b], l + 1)
                    dve.wait_ge(xb_ready[b], 2 * l + 2)
                    nc.vector.tensor_tensor(x[b][:], pa[b][:, 0:NT * D].rearrange("p (t d) -> p t d", t=NT), xb[b][:],
                                            ALU.add).then_inc(x_ready[b], 1)
                elif stage == "head":
                    dve.wait_ge(x_ready[b], 2 * LAYERS + 1)
                    norm_stats(b, LNF, x[b], D, NT, EPS)
                    normalise(b, LNF, xn[b], x[b], D, NT).then_inc(xn_ready[b], 1)
                    dve.wait_ge(head_done[b], 1)
                    link(nc.vector.tensor_tensor(h[b][:, 0:NT, :],
                                                 pb[b][:].rearrange("p (t w) -> p t w", t=NT)[:, :, 0:W],
                                                 rows[:, ROW_HEADB:ROW_HEADB + W].unsqueeze(1).to_broadcast([P, NT, W]),
                                                 ALU.add))
                elif stage == "scan_in":
                    norm_stats(b, LN_SCAN, h[b], W, 3, EPS)
                    link(normalise(b, LN_SCAN, hn[b], h[b], W, 3))
                    for t in range(3):
                        last = nc.vector.tensor_copy(hn[b][0:ROWS[t], t, W:2 * P], hn[b][0:ROWS[t], t, P:W])
                    last.then_inc(xn_ready[b], 1)
                    dve.wait_ge(bcd_done[b], 1)
                    for c in range(2):
                        last = nc.vector.tensor_scalar(z[b][:, c, :], pb[b][:, BANK:BANK + L], pdelta[:, c:c + 1], None,
                                                       ALU.add)
                    last.then_inc(z_ready[b], 1)
                    dve.wait_ge(bc_ready[b], 1)
                    K = 2 * N
                    link(nc.vector.tensor_copy(bc3[b][0:K, :], bc[b][:]))
                    link(nc.vector.tensor_tensor(bcr[b][:], bc[b][:], bc3[b][0:K, :], ALU.subtract))
                    link(nc.vector.tensor_copy(bc3[b][K:2 * K, :], bcr[b][:]))
                    link(nc.vector.tensor_copy(bc[b][:], bc3[b][K:2 * K, :]))
                    link(nc.vector.tensor_tensor(bcr[b][:], bcr[b][:], bc[b][:], ALU.subtract))
                    nc.vector.tensor_copy(bc3[b][2 * K:3 * K, :], bcr[b][:]).then_inc(bc3_ready[b], 1)
                    dve.wait_ge(lnz_ready[b], 1)
                    nc.vector.scalar_tensor_tensor(delta[b][:], z[b][:], 0.0, ez[b][:], ALU.max,
                                                   ALU.add).then_inc(delta_ready[b], 1)
                elif stage == "scan":
                    scan_chunks(b)
                elif stage == "scan_out":
                    dve.wait_ge(yback_done[b], 1)
                    nc.vector.tensor_tensor(h[b][:, 0:NT, :], h[b][:, 0:NT, :],
                                            pb[b][:, 0:NT * W].rearrange("p (t w) -> p t w", t=NT), ALU.add)
                    link(nc.vector.tensor_tensor(h[b][0:S_TXT, NT, :], h[b][0:S_TXT, NT, :],
                                                 pb[b][0:S_TXT, BANK:BANK + W], ALU.add))
                elif stage == "ffn":
                    norm_stats(b, LN_FFN, h[b], W, 3, EPS)
                    normalise(b, LN_FFN, hn[b], h[b], W, 3).then_inc(xn_ready[b], 1)
                    dve.wait_ge(fout_done[b], 1)
                    bo = rows[:, ROW_BO:ROW_BO + W]
                    nc.vector.tensor_tensor(o[b][:, 0:NT, :], pb[b][:, 0:NT * W].rearrange("p (t w) -> p t w", t=NT),
                                            bo.unsqueeze(1).to_broadcast([P, NT, W]), ALU.add)
                    link(nc.vector.tensor_tensor(o[b][0:S_TXT, NT, :], pb[b][0:S_TXT, BANK:BANK + W], bo[0:S_TXT, :],
                                                 ALU.add))
                    norm_stats(b, LN_OUT, o[b], W, 3, EPS)
                    fb, fg = rows[:, ROW_FB:ROW_FB + W], rows[:, ROW_FG:ROW_FG + W]
                    nc.vector.tensor_tensor(h[b][:, 0:NT, :], h[b][:, 0:NT, :],
                                            fb.unsqueeze(1).to_broadcast([P, NT, W]), ALU.add)
                    nc.vector.tensor_tensor(h[b][0:S_TXT, NT, :], h[b][0:S_TXT, NT, :], fb[0:S_TXT, :], ALU.add)
                    link(normalise(b, LN_OUT, o[b], o[b], W, 3))
                    nc.vector.tensor_tensor(o[b][:, 0:NT, :], o[b][:, 0:NT, :],
                                            fg.unsqueeze(1).to_broadcast([P, NT, W]), ALU.mult)
                    link(nc.vector.tensor_tensor(o[b][0:S_TXT, NT, :], o[b][0:S_TXT, NT, :], fg[0:S_TXT, :], ALU.mult))
                    nc.vector.tensor_tensor(o[b][:, 0:NT, :], o[b][:, 0:NT, :], h[b][:, 0:NT, :], ALU.add)
                    nc.vector.tensor_tensor(o[b][0:S_TXT, NT, :], o[b][0:S_TXT, NT, :], h[b][0:S_TXT, NT, :],
                                            ALU.add).then_inc(o_ready[b], 1)

        @block.scalar
        def _(act):
            steps = [0]

            def link(ins):
                steps[0] += 1
                ins.then_inc(act_step, 1)
                act.wait_ge(act_step, steps[0])

            def affine(b, i, c):
                act.wait_ge(tr_done[b], i + 1)
                nc.scalar.activation(yt[b][:], pa[b][:, 0:TOK], ACT.Identity, bias=col(c + 1),
                                     scale=col(c)).then_inc(yt_ready[b], 1)

            act.wait_ge(s_cols, 16)
            act.wait_ge(s_txtconv, NB)
            for b in range(NB):
                last = nc.scalar.activation(txt[:, b, :], pb[b][0:S_TXT, 0:W], ACT.Gelu)
            last.then_inc(s_txtgelu, 1)
            nc.scalar.preload_act_table(ACT.Exp)

            for stage, b, l in STAGES:
                if stage == "att_norm":
                    affine(b, 2 * l, COL_LN + 4 * l)
                elif stage == "att_in":
                    act.wait_ge(kmax_ready[b], l + 1)
                    for j in range(NJ):
                        last = nc.scalar.activation(ekt[b][:, j, :], pb[b][:, j * TOK:(j + 1) * TOK], ACT.Exp,
                                                    bias=kmax[b][:, j:j + 1], accum_out=ksum[b][:, j:j + 1])
                    last.then_inc(ek_ready[b], 1)
                    act.wait_ge(qsub_ready[b], l + 1)
                    nc.scalar.activation(q[b][:], q[b][:], ACT.Exp).then_inc(eq_ready[b], 1)
                    act.wait_ge(v_done[b], l + 1)
                    nc.scalar.activation(v[b][:].rearrange("p t w -> p (t w)"), pb[b][:],
                                         ACT.Copy).then_inc(v_ready[b], 1)
                elif stage == "att_mid":
                    act.wait_ge(kn_done[b], l + 1)
                    nc.scalar.activation(kn[b][:].rearrange("p t w -> p (t w)"), pa[b][:],
                                         ACT.Copy).then_inc(kn_ready[b], 1)
                    act.wait_ge(qt_done[b], l + 1)
                    nc.scalar.activation(qt[b][:].rearrange("p j n -> p (j n)"), pb[b][:],
                                         ACT.Copy).then_inc(qt_ready[b], 1)
                elif stage == "ff_norm":
                    affine(b, 2 * l + 1, COL_LN + 4 * l + 2)
                elif stage == "ff":
                    act.wait_ge(ff1_done[b], l + 1)
                    for k in range(NM):
                        last = nc.scalar.activation(hid[b][:, k, :], pb[b][:, k * TOK:(k + 1) * TOK], ACT.Gelu,
                                                    bias=col(COL_FF1B + NM * l + k))
                    last.then_inc(gelu_done[b], 1)
                    if b == NB - 1:
                        if l < LAYERS - 1:
                            nc.scalar.preload_act_table(ACT.Exp)
                        else:
                            nc.scalar.preload_act_table_set("natural_log_exp_and_others")
                elif stage == "head":
                    affine(b, LNF, COL_LNF)
                elif stage == "scan_in":
                    act.wait_ge(tr_done[b], LN_SCAN + 1)
                    nc.scalar.activation(ht[b][:], pa[b][:].rearrange("p (c n) -> p c n", c=2)[:, :, 0:L],
                                         ACT.Copy).then_inc(yt_ready[b], 1)
                    act.wait_ge(bcd_done[b], 1)
                    nc.scalar.activation(bc[b][:], pb[b][0:2 * N, 0:L], ACT.Identity,
                                         bias=col(COL_BBC, 1, 2 * N)).then_inc(bc_ready[b], 1)
                    act.wait_ge(z_ready[b], 1)
                    link(nc.scalar.activation(ez[b][:], z[b][:], ACT.Abs))
                    link(nc.scalar.activation(ez[b][:], ez[b][:], ACT.Exp, scale=-1.0))
                    nc.scalar.activation(ez[b][:], ez[b][:], ACT.Ln, bias=1.0).then_inc(lnz_ready[b], 1)
                elif stage == "scan":
                    act.wait_ge(delta_ready[b], 1)
                    for c in range(NC_):
                        g = b * NC_ + c
                        if g >= RA:
                            act.wait_ge(hs_ready, g - RA + 1)
                        nc.scalar.activation(abar[:, g % RA, :], delta[b][:, 0 if c < C0 else 1, :], ACT.Exp,
                                             scale=col(COL_A + c)).then_inc(abar_ready, 1)
                elif stage == "scan_out":
                    act.wait_ge(m_summed, (b + 1) * NC_)
                    nc.scalar.activation(ys[b][:, 0, :], pa[b][:, 0:L], ACT.Copy)
                    nc.scalar.activation(ys[b][0:W1, 1, :], pa[b][0:W1, BANK:BANK + L],
                                         ACT.Copy).then_inc(ys_ready[b], 1)
                elif stage == "ffn":
                    act.wait_ge(tr_done[b], LN_FFN + 1)
                    nc.scalar.activation(ht[b][:, 0, :], pa[b][:, 0:L], ACT.Copy)
                    nc.scalar.activation(ht[b][0:W1, 1, :], pa[b][0:W1, BANK:BANK + L],
                                         ACT.Copy).then_inc(yt_ready[b], 1)
                    act.wait_ge(fhid_done[b], 1)
                    nc.scalar.activation(fhid[b][:], pb[b][:, 0:L], ACT.Relu,
                                         bias=col(COL_B1)).then_inc(fhid_ready[b], 1)
                    act.wait_ge(fpred_done[b], 1)
                    nc.scalar.activation(fpred[b][:, 0, :], pa[b][:, 0:L], ACT.Identity, bias=col(COL_B2))
                    nc.scalar.activation(fpred[b][0:W1, 1, :], pa[b][0:W1, BANK:BANK + L], ACT.Identity,
                                         bias=col(COL_B2 + 1, 1, W1)).then_inc(fpred_ready[b], 1)

        @block.tensor
        def _(pe):
            def mm(dst, lhs_t, rhs, first=True, last=True):
                return nc.tensor.matmul(dst, lhs_t, rhs, start=first, stop=last)

            def to_features(b, i):
                pe.wait_ge(xn_ready[b], i + 1)
                for t in range(NT):
                    last = nc.tensor.transpose(pa[b][:, t * P:(t + 1) * P], xn[b][:, t, :], ident[:])
                last.then_inc(tr_done[b], 1)

            def h_to_features(b, i, second):
                pe.wait_ge(xn_ready[b], i + 1)
                for t in range(3):
                    r = ROWS[t]
                    nc.tensor.transpose(pa[b][:, t * P:t * P + r], hn[b][0:r, t, 0:P], ident[0:r, 0:r])
                    last = nc.tensor.transpose(pa[b][0:second, BANK + t * P:BANK + t * P + r],
                                               hn[b][0:r, t, P:P + second], ident[0:r, 0:r])
                last.then_inc(tr_done[b], 1)

            pe.wait_ge(s_band, 1)
            pe.wait_ge(s_edges, 1)
            pe.wait_ge(s_pos, 16 * NB)
            pe.wait_ge(s_word, 16)
            for b in range(NB):
                for k in range(6):
                    src = we if k < 3 else pe_rows
                    last = mm(pb[b][0:S_TXT, 0:W], band[:, k, b * S_TXT:(b + 1) * S_TXT],
                              src[:, k % 3:k % 3 + W], k == 0, k == 5)
                last.then_inc(s_txtconv, 1)
            pe.wait_ge(s_txtgelu, 1)
            pe.wait_ge(s_ident, 16)

            for stage, b, l in STAGES:
                if stage == "conv":
                    for g in range(KT // KG):
                        pe.wait_ge(s_convw[g], 16)
                        pe.wait_ge(s_patch[b][g], 16)
                        for k in range(g * KG, (g + 1) * KG):
                            for t in range(NT):
                                last = mm(pa[b][:, t * BANK:t * BANK + D], patch_sb[b][:, k, t * P:(t + 1) * P],
                                          convw_sb[:, k, :], k == 0, k == KT - 1)
                    last.then_inc(conv_done[b], 1)
                elif stage == "att_norm":
                    to_features(b, 2 * l)
                elif stage == "att_in":
                    pe.wait_ge(yt_ready[b], 2 * l + 1)
                    pe.wait_ge(s_qkv, 16)
                    for j in range(NJ):
                        last = mm(pb[b][:, j * TOK:(j + 1) * TOK], qkv_sb[:, l, INNER + j * P:INNER + (j + 1) * P],
                                  yt[b][:])
                    last.then_inc(kt_done[b], 1)
                    for t in range(NT):
                        last = mm(pa[b][:, t * BANK:(t + 1) * BANK], yt[b][:, t * P:(t + 1) * P], qkv_sb[:, l, 0:INNER])
                    last.then_inc(q_done[b], 1)
                    pe.wait_ge(ek_ready[b], l + 1)
                    for t in range(NT):
                        last = mm(pb[b][:, t * BANK:(t + 1) * BANK], yt[b][:, t * P:(t + 1) * P],
                                  qkv_sb[:, l, 2 * INNER:3 * INNER])
                    last.then_inc(v_done[b], 1)
                elif stage == "att_mid":
                    pe.wait_ge(qsub_ready[b], l + 1)
                    for t in range(NT):
                        for j in range(NJ):
                            last = nc.tensor.transpose(pa[b][:, t * BANK + j * P:t * BANK + (j + 1) * P],
                                                       ekt[b][:, j, t * P:(t + 1) * P], ident[:])
                    last.then_inc(kn_done[b], 1)
                    pe.wait_ge(qn_ready[b], l + 1)
                    pe.wait_ge(v_ready[b], l + 1)
                    qv = q[b][:].rearrange("p (t e) d -> p t (e d)", t=NT)
                    for j in range(NJ):
                        for t in range(NT):
                            last = nc.tensor.transpose(pb[b][:, j * TOK + t * P:j * TOK + (t + 1) * P],
                                                       qv[:, t, j * P:(j + 1) * P], ident[:])
                    last.then_inc(qt_done[b], 1)
                elif stage == "att_out":
                    pe.wait_ge(kn_ready[b], l + 1)
                    for j in range(NJ):
                        for t in range(NT):
                            last = mm(pa[b][:, j * P:(j + 1) * P], v[b][:, t, j * P:(j + 1) * P],
                                      kn[b][:, t, j * P:(j + 1) * P], t == 0, t == NT - 1)
                    last.then_inc(ctx_done[b], 1)
                    pe.wait_ge(ctx_ready[b], l + 1)
                    pe.wait_ge(s_outw, 16)
                    for j in range(NJ):
                        last = mm(pa[b][:, BANK + j * D:BANK + (j + 1) * D], ctxt[b][:, j, :], outw_sb[:, l, j, :])
                    last.then_inc(cw_done[b], 1)
                    pe.wait_ge(cw_ready[b], l + 1)
                    pe.wait_ge(qt_ready[b], l + 1)
                    for t in range(NT):
                        for j in range(NJ):
                            last = mm(pb[b][:, t * D:(t + 1) * D], qt[b][:, j, t * P:(t + 1) * P], cw[b][:, j, :],
                                      j == 0, j == NJ - 1)
                    last.then_inc(att_done[b], 1)
                elif stage == "ff_norm":
                    to_features(b, 2 * l + 1)
                elif stage == "ff":
                    pe.wait_ge(yt_ready[b], 2 * l + 2)
                    pe.wait_ge(s_ff1, 16)
                    for k in range(NM):
                        last = mm(pb[b][:, k * TOK:(k + 1) * TOK], ff1_sb[:, l, k * P:(k + 1) * P], yt[b][:])
                    last.then_inc(ff1_done[b], 1)
                    pe.wait_ge(gelu_done[b], l + 1)
                    pe.wait_ge(s_ff2, 16)
                    for t in range(NT):
                        for k in range(NM):
                            last = mm(pa[b][:, t * D:(t + 1) * D], hid[b][:, k, t * P:(t + 1) * P], ff2_sb[:, l, k, :],
                                      k == 0, k == NM - 1)
                    last.then_inc(ff2_done[b], 1)
                elif stage == "head":
                    to_features(b, LNF)
                    pe.wait_ge(yt_ready[b], LNF + 1)
                    pe.wait_ge(s_misc, 16)
                    for t in range(NT):
                        last = mm(pb[b][:, t * BANK:t * BANK + W], yt[b][:, t * P:(t + 1) * P],
                                  misc[:, MI_HEAD:MI_HEAD + W])
                    last.then_inc(head_done[b], 1)
                elif stage == "scan_in":
                    h_to_features(b, LN_SCAN, P)
                    pe.wait_ge(yt_ready[b], LN_SCAN + 1)
                    for c in range(2):
                        r = parts(c)
                        mm(pb[b][0:2 * N, 0:L], misc[0:r, MI_BC + 2 * N * c:MI_BC + 2 * N * (c + 1)], ht[b][0:r, c, :],
                           c == 0, c == 1)
                    for c in range(2):
                        r = parts(c)
                        last = mm(pb[b][:, BANK:BANK + L], misc[0:r, MI_WD + P * c:MI_WD + P * (c + 1)],
                                  ht[b][0:r, c, :], c == 0, c == 1)
                    last.then_inc(bcd_done[b], 1)
                elif stage == "scan":
                    pe.wait_ge(bc3_ready[b], 1)
                    pe.wait_ge(s_sel, 16)
                    pe.wait_ge(z_ready[b], 1)

                    def spread_b(c):
                        if c:
                            pe.wait_ge(u_ready, b * NC_ + c)
                        mm(pb[b][:, 0:L], sel[:, 2 * c, :], bc3[b][:]).then_inc(b_spread, 1)

                    def spread_c(c):
                        if c:
                            pe.wait_ge(m_ready, b * NC_ + c)
                        mm(pb[b][:, BANK:BANK + L], sel[:, 2 * c + 1, :], bc3[b][:]).then_inc(c_spread, 1)

                    def sum_m(c):
                        pe.wait_ge(m_ready, b * NC_ + c + 1)
                        src = m[:, (b * NC_ + c) % RM, :]
                        if c < C0:
                            mm(pa[b][:, 0:L], ident[:], src, c == 0, c == C0 - 1).then_inc(m_summed, 1)
                        else:
                            mm(pa[b][0:W1, BANK:BANK + L], misc[:, MI_FOLD:MI_FOLD + W1], src, c == C0,
                               c == NC_ - 1).then_inc(m_summed, 1)

                    spread_b(0)
                    spread_c(0)
                    for c in range(1, NC_):
                        spread_b(c)
                        if c >= 2:
                            spread_c(c - 1)
                            sum_m(c - 2)
                    spread_c(NC_ - 1)
                    sum_m(NC_ - 2)
                    sum_m(NC_ - 1)
                elif stage == "scan_out":
                    pe.wait_ge(ys_ready[b], 1)
                    for t in range(3):
                        r = ROWS[t]
                        base = t * W if t < NT else BANK
                        nc.tensor.transpose(pb[b][0:r, base:base + P], ys[b][:, 0, t * P:t * P + r], ident[:])
                        last = nc.tensor.transpose(pb[b][0:r, base + P:base + W], ys[b][0:W1, 1, t * P:t * P + r],
                                                   ident[0:W1, 0:W1])
                    last.then_inc(yback_done[b], 1)
                elif stage == "ffn":
                    h_to_features(b, LN_FFN, W1)
                    pe.wait_ge(yt_ready[b], LN_FFN + 1)
                    for c in range(2):
                        r = parts(c)
                        last = mm(pb[b][:, 0:L], misc[0:r, MI_W1 + FFI * c:MI_W1 + FFI * (c + 1)], ht[b][0:r, c, :],
                                  c == 0, c == 1)
                    last.then_inc(fhid_done[b], 1)
                    pe.wait_ge(fhid_ready[b], 1)
                    mm(pa[b][:, 0:L], misc[:, MI_W2:MI_W2 + P], fhid[b][:])
                    mm(pa[b][0:W1, BANK:BANK + L], misc[:, MI_W2 + P:MI_W2 + W], fhid[b][:]).then_inc(fpred_done[b], 1)
                    pe.wait_ge(fpred_ready[b], 1)
                    for t in range(3):
                        r = ROWS[t]
                        base = t * W if t < NT else BANK
                        for c in range(2):
                            k = parts(c)
                            last = mm(pb[b][0:r, base:base + W], fpred[b][0:k, c, t * P:t * P + r],
                                      misc[0:k, MI_WO + W * c:MI_WO + W * (c + 1)], c == 0, c == 1)
                    last.then_inc(fout_done[b], 1)


def kernel(**inputs):
    import concourse.bacc as bacc
    import ml_dtypes
    from concourse.bass_utils import run_bass_kernel_spmd

    a = {k: np.asarray(x) for k, x in inputs.items()}
    f32 = np.float32

    def two_parts(w):
        second = np.zeros((P, w.shape[1]), f32)
        second[:W1] = w[P:]
        return np.concatenate([w[:P], second], axis=1)

    def column(v, rows=P):
        c = np.zeros((P, 1), f32)
        c[:rows, 0] = v
        return c

    x = a["x"].reshape(NB, 32, 16, 8, 16, 8)
    patches = x.transpose(0, 1, 3, 5, 2, 4).reshape(NB, KT, P, TOK).transpose(0, 2, 1, 3)
    convw = a["L0_tok_conv_w"].reshape(D, KT, P).transpose(2, 1, 0)
    qkvw = a["L0_tok_qkv_w"].transpose(1, 0, 2)
    outw = a["L0_tok_out_w"].reshape(LAYERS, NJ, P, D).transpose(2, 0, 1, 3)
    ff1w = a["L0_tok_ff1_w"].transpose(1, 0, 2)
    ff2w = a["L0_tok_ff2_w"].reshape(LAYERS, NM, P, D).transpose(2, 0, 1, 3)

    cols = []
    for l in range(LAYERS):
        for n in ("ln1_g", "ln1_b", "ln2_g", "ln2_b"):
            cols.append(column(a["L0_tok_" + n][l]))
    cols += [column(a["L0_tok_lnf_g"]), column(a["L0_tok_lnf_b"])]
    cols.append(a["L0_tok_ff1_b"].reshape(LAYERS * NM, P).T)
    cols.append(column(np.concatenate([a["L0_attn_b_B"], a["L0_attn_b_C"]]), 2 * N))
    cols.append(column(a["L0_ffn_b1"]))
    cols += [column(a["L0_ffn_b2"][:P]), column(a["L0_ffn_b2"][P:], W1)]
    pd = a["L0_attn_p_Delta"]
    cols += [column(pd[:P]), column(np.tile(pd[P:], 2))]
    cols.append(np.broadcast_to(a["L0_attn_b_D"].reshape(1, 1), (P, 1)))
    aa = a["L0_attn_A"]
    cols.append(aa[:P])
    cols.append(np.concatenate([aa[P:, :C1], aa[P:, C1:]], axis=0))
    taps = a["L0_txt_conv_w"][0].transpose(1, 0, 2).reshape(1, 18)
    cols.append(np.broadcast_to(taps, (P, 18)))
    cols = np.ascontiguousarray(np.concatenate(cols, axis=1))
    assert cols.shape == (P, NCOLS)

    rows = np.concatenate([
        a["L0_tok_conv_b"], a["L0_tok_out_b"].ravel(), a["L0_tok_ff2_b"].ravel(), a["L0_tok_head_b"],
        a["L0_ffn_bo"], a["L0_ffn_gamma"], a["L0_ffn_beta"], a["L0_txt_ln_gamma"], a["L0_txt_ln_beta"]])
    assert rows.shape == (NROWS,)

    w_bc = np.concatenate([a["L0_attn_W_B"], a["L0_attn_W_C"]], axis=1)
    fold = np.zeros((P, W1), f32)
    fold[np.arange(P), np.arange(P) % W1] = 1.0
    misc = np.concatenate([
        a["L0_tok_head_w"], two_parts(w_bc), two_parts(np.broadcast_to(a["L0_attn_W_D"], (W, P))),
        two_parts(a["L0_ffn_W1"].T), a["L0_ffn_W2"].T, two_parts(a["L0_ffn_Wo"].T), fold], axis=1)
    assert misc.shape == (P, NMISC)

    shifts = np.zeros((2 * S_TXT, 3, 2 * S_TXT), f32)
    for i in range(3):
        for s in range(2 * S_TXT):
            if 0 <= s % S_TXT + i - 1 < S_TXT:
                shifts[s + i - 1, i, s] = 1.0
    sel = np.zeros((3, 2 * N, NC_, 2, P), f32)
    for c in range(NC_):
        states = [c, c] if c < C0 else [c - C0, c - C0 + C1]
        for half, n in enumerate(states):
            cut = slice(half * W1, (half + 1) * W1)
            sel[:, n, c, 0, cut] = 1.0
            sel[:, N + n, c, 1, cut] = 1.0
    arrays = {
        "ids": a["x_txt"].astype(np.int32).reshape(2 * S_TXT, 1),
        "patches": patches, "convw": convw, "qkvw": qkvw, "outw": outw, "ff1w": ff1w, "ff2w": ff2w,
        "cols": cols, "rows": rows, "misc": misc, "ident": np.eye(P, dtype=f32),
        "tconst": shifts.reshape(2 * S_TXT, NTC),
        "sel": sel.reshape(3 * 2 * N, 2 * NC_, P).astype(ml_dtypes.bfloat16),
        "word_emb": a["L0_txt_word_emb"], "pos_emb": a["L0_txt_pos_emb"],
    }
    nc = bacc.Bacc("TRN2", target_bir_lowering=False, num_devices=1)
    laid, args = {}, []
    for name, arr in arrays.items():
        arr = np.ascontiguousarray(arr)
        laid[f"in_{name}"] = arr
        args.append(nc.dram_tensor(f"in_{name}", arr.shape, mybir.dt.from_np(arr.dtype), kind="ExternalInput").ap())
    args.append(nc.dram_tensor("out", (NB, L, W), F32, kind="ExternalOutput").ap())
    build(nc, *args)
    r = run_bass_kernel_spmd(nc, [laid], core_ids=[0])
    return r.results[0]["out"]
```

```python
from contextlib import ExitStack

import numpy as np

import concourse.bass as bass
from concourse import mybir

F32 = mybir.dt.float32
BF16 = mybir.dt.bfloat16
I32 = mybir.dt.int32
ALU = mybir.AluOpType
ACT = mybir.ActivationFunctionType
AX = mybir.AxisListType.X

P = 128
NB = 2
D = 128
NT = 2
TOK = NT * P
KT = 16
KG = 4
LAYERS = 2
NH, DH = 8, 64
INNER = NH * DH
NJ = INNER // P
M = 512
NM = M // P
W = 192
W1 = W - P
S_TXT = 32
L = TOK + S_TXT
ROWS = [P, P, S_TXT]
N = 16
C0, C1 = N, N // 2
NC_ = C0 + C1
BANK = 512
FFI = 128
BEHIND = 2

COL_LN = 0
COL_LNF = COL_LN + 4 * LAYERS
COL_FF1B = COL_LNF + 2
COL_BBC = COL_FF1B + NM * LAYERS
COL_B1 = COL_BBC + 1
COL_B2 = COL_B1 + 1
COL_PD = COL_B2 + 2
COL_BD = COL_PD + 2
COL_A = COL_BD + 1
COL_CW = COL_A + NC_
NCOLS = COL_CW + 18
ROW_CONVB = 0
ROW_OUTB = ROW_CONVB + D
ROW_FF2B = ROW_OUTB + LAYERS * D
ROW_HEADB = ROW_FF2B + LAYERS * D
ROW_BO = ROW_HEADB + W
ROW_FG = ROW_BO + W
ROW_FB = ROW_FG + W
ROW_TG = ROW_FB + W
ROW_TB = ROW_TG + W
NROWS = ROW_TB + W
MI_HEAD = 0
MI_BC = MI_HEAD + W
MI_WD = MI_BC + 2 * 2 * N
MI_W1 = MI_WD + 2 * P
MI_W2 = MI_W1 + 2 * FFI
MI_WO = MI_W2 + W
MI_FOLD = MI_WO + 2 * W
NMISC = MI_FOLD + W1
TC_SHIFT = 0
NTC = 3 * 2 * S_TXT

EPS = 1e-5
EPS_TXT = 1e-12


def build(nc, ids, patches, convw, qkvw, outw, ff1w, ff2w, cols_d, rows_d, misc_d, ident_d, tconst_d,
          sel_d, word_emb, pos_emb, out):
    ctx = ExitStack()
    with ctx:
        def sb(name, shape, dt=F32):
            return ctx.enter_context(nc.sbuf_tensor(name, shape, dt))

        def sem(name):
            return ctx.enter_context(nc.semaphore(name))

        def per_batch(make, name):
            return [make(f"{name}_{b}") for b in range(NB)]

        patch_sb = [sb(f"patch_{b}", [P, KT, TOK]) for b in range(NB)]
        convw_sb = sb("convw", [P, KT, D])
        qkv_sb = sb("qkvw", [P, LAYERS, 3 * INNER])
        outw_sb = sb("outw", [P, LAYERS, NJ, D])
        ff1_sb = sb("ff1w", [P, LAYERS, M])
        ff2_sb = sb("ff2w", [P, LAYERS, NM, D])
        cols = sb("cols", [P, NCOLS])
        rows = sb("rows", [P, NROWS])
        misc = sb("misc", [P, NMISC])
        ident = sb("ident", [P, P])
        tconst = sb("tconst", [2 * S_TXT, NTC])
        sel = sb("sel", [3 * 2 * N, 2 * C0 + 2 * C1, P], BF16)
        ids_sb = sb("ids", [2 * S_TXT, 1], I32)
        neghalf = sb("neghalf", [P, 4])
        inv_a = sb("inv_a", [P, NC_])
        sum0 = sb("sum_lower", [P, C0, P])
        sum1 = sb("sum_upper", [P, C1, W1])
        pdelta = sb("pdelta", [P, 2])
        we = sb("word_rows", [2 * S_TXT, W + 2])
        pe_rows = sb("pos_rows", [2 * S_TXT, W + 2])
        band = sb("band", [2 * S_TXT, 6, 2 * S_TXT])
        band_t = sb("band_term", [2 * S_TXT, 6, 2 * S_TXT])
        txt = sb("txt", [S_TXT, NB, W])
        tstats, tmv = sb("txt_stats", [S_TXT, NB, 6]), sb("txt_mean_var", [S_TXT, NB, 2])
        tve, trstd = sb("txt_var_eps", [S_TXT, NB]), sb("txt_rstd", [S_TXT, NB])
        x = per_batch(lambda n: sb(n, [P, NT, D]), "x")
        xb = per_batch(lambda n: sb(n, [P, NT, D]), "x_plus_bias")
        xn = per_batch(lambda n: sb(n, [P, NT, D]), "x_normed")
        yt = per_batch(lambda n: sb(n, [P, TOK]), "y_t")
        stats = per_batch(lambda n: sb(n, [P, 3, 6]), "stats")
        mv = per_batch(lambda n: sb(n, [P, 3, 2]), "mean_var")
        ve = per_batch(lambda n: sb(n, [P, 3]), "var_eps")
        rstd = per_batch(lambda n: sb(n, [P, 3]), "rstd")
        kmax = per_batch(lambda n: sb(n, [P, NJ]), "neg_kmax")
        ksum = per_batch(lambda n: sb(n, [P, NJ]), "ksum")
        krec = per_batch(lambda n: sb(n, [P, NJ]), "krec")
        ekt = per_batch(lambda n: sb(n, [P, NJ, TOK]), "exp_k_t")
        kn = per_batch(lambda n: sb(n, [P, NT, INNER]), "exp_k")
        v = per_batch(lambda n: sb(n, [P, NT, INNER]), "v")
        qmax = per_batch(lambda n: sb(n, [P, NT * NH]), "qmax")
        qrec = per_batch(lambda n: sb(n, [P, NT * NH]), "qrec")
        q = per_batch(lambda n: sb(n, [P, NT * NH, DH]), "q")
        qt = per_batch(lambda n: sb(n, [P, NJ, TOK]), "q_t")
        ctxt = per_batch(lambda n: sb(n, [P, NJ, P]), "ctx_t")
        cw = per_batch(lambda n: sb(n, [P, NJ, D]), "ctx_outw")
        hid = ekt
        h = per_batch(lambda n: sb(n, [P, 3, W]), "h")
        hn = per_batch(lambda n: sb(n, [P, 3, 2 * P]), "h_normed")
        ht = per_batch(lambda n: sb(n, [P, 2, L]), "h_t")
        bc = per_batch(lambda n: sb(n, [2 * N, L]), "bc")
        bcr = per_batch(lambda n: sb(n, [4 * N, L]), "bc_rest")
        bc3 = per_batch(lambda n: sb(n, [3 * 2 * N, L], BF16), "bc_parts")
        z = per_batch(lambda n: sb(n, [P, 2, L]), "z_above_zero")
        ez = per_batch(lambda n: sb(n, [P, 2, L]), "exp_z")
        delta = per_batch(lambda n: sb(n, [P, 2, L]), "delta")
        ys = ez
        fhid = per_batch(lambda n: sb(n, [P, L]), "ffn_hidden")
        fpred = z
        o = per_batch(lambda n: sb(n, [P, 3, W]), "o")
        RA, RB, RH, RM, RU = 6, 2, 2, 4, 3
        flat = [patch_sb[b][:].rearrange("p k n -> p (k n)") for b in range(NB)]
        flat_w = convw_sb[:].rearrange("p k n -> p (k n)")

        def ring(src, first, n):
            return src[:, first * L:(first + n) * L].rearrange("p (r n) -> p r n", r=n)

        abar = [ring(flat[b], 0, RA) for b in range(NB)]
        binc = [ring(flat[b], RA, RB) for b in range(NB)]
        hs = [ring(flat[b], RA + RB, RH) for b in range(NB)]
        m = [ring(flat[b], RA + RB + RH, RM) for b in range(NB)]
        u = [ring(flat_w, b * RU, RU) for b in range(NB)]
        bsp = [ring(kn[b][:].rearrange("p t w -> p (t w)"), 0, 2) for b in range(NB)]

        pa = [ctx.enter_context(nc.psum_tensor(f"pa_{b}", [P, 2 * BANK], F32)) for b in range(NB)]
        pb = [ctx.enter_context(nc.psum_tensor(f"pb_{b}", [P, 2 * BANK], F32)) for b in range(NB)]

        s_ids = sem("ids_loaded")
        s_patch0 = [sem(f"patch_0_and_convw_loaded_{g}") for g in range(KT // KG)]
        s_patch1 = sem("patch_1_loaded")
        s_cols, s_rows, s_rows2, s_misc, s_ident = sem("cols_loaded"), sem("rows_loaded"), sem("late_rows_loaded"), sem("misc_loaded"), sem("ident_loaded")
        s_tconst, s_pos, s_word, s_sel = sem("tconst_loaded"), sem("pos_loaded"), sem("words_gathered"), sem("sel_loaded")
        s_qkv, s_outw = ([sem(f"{n}_loaded_{l}") for l in range(LAYERS)]
                                       for n in ("qkvw", "outw_ff1w_ff2w"))
        s_out = sem("out_written")
        s_fill, s_edges = sem("pool_fills_done"), sem("edges_zeroed")
        s_band, s_txtconv, s_txtgelu = sem("band_ready"), sem("txt_conv_done"), sem("txt_gelu_done")
        s_txtvar, s_txtrstd = sem("txt_var_ready"), sem("txt_rstd_ready")
        dve_step = sem("dve_step")
        act_step = sem("act_step")
        conv_done = per_batch(sem, "conv_done")
        x_ready = per_batch(sem, "x_ready")
        xb_ready = per_batch(sem, "x_plus_bias_ready")
        var_ready = per_batch(sem, "var_ready")
        rstd_ready = per_batch(sem, "rstd_ready")
        xn_ready = per_batch(sem, "normed_ready")
        tr_done = per_batch(sem, "normed_transposed")
        yt_ready = per_batch(sem, "normed_t_ready")
        kt_done = per_batch(sem, "k_done")
        q_done = per_batch(sem, "q_done")
        v_done = per_batch(sem, "v_done")
        kmax_ready = per_batch(sem, "kmax_ready")
        ek_ready = per_batch(sem, "exp_k_ready")
        qsub_ready = per_batch(sem, "q_shifted")
        eq_ready = per_batch(sem, "exp_q_ready")
        qn_ready = per_batch(sem, "q_normed")
        v_ready = per_batch(sem, "v_copied")
        kn_done = per_batch(sem, "exp_k_transposed")
        kn_ready = per_batch(sem, "exp_k_copied")
        qt_done = per_batch(sem, "q_transposed")
        qt_ready = per_batch(sem, "q_t_copied")
        ctx_done = per_batch(sem, "ctx_done")
        ctx0_ready = per_batch(sem, "ctx_even_heads_copied")
        ctx1_ready = per_batch(sem, "ctx_odd_heads_copied")
        cw_done = per_batch(sem, "ctx_outw_done")
        cw_ready = per_batch(sem, "ctx_outw_copied")
        att_done = per_batch(sem, "att_done")
        ff1_done = per_batch(sem, "ff1_done")
        gelu_done = per_batch(sem, "gelu_done")
        ff2_done = per_batch(sem, "ff2_done")
        head_done = per_batch(sem, "head_done")
        bcd_done = per_batch(sem, "bc_delta_products_done")
        bc_ready = per_batch(sem, "bc_copied")
        z_read = per_batch(sem, "z_read")
        zabs_ready = per_batch(sem, "abs_z_ready")
        sums_ready = sem("sum_matrices_ready")
        inv_ready = sem("inv_a_ready")
        pdelta_ready = sem("pdelta_ready")
        bc1_ready = per_batch(sem, "bc_first_part_ready")
        lnz_ready = per_batch(sem, "ln_exp_ready")
        bc3_ready = per_batch(sem, "bc_parts_ready")
        delta_ready = per_batch(sem, "delta_ready")
        b_spread = per_batch(sem, "b_spread")
        b_copied = per_batch(sem, "b_copied")
        c_spread = per_batch(sem, "c_spread")
        abar_ready = per_batch(sem, "a_bar_ready")
        u_ready = per_batch(sem, "u_ready")
        binc_ready = per_batch(sem, "b_inc_ready")
        hs_ready = per_batch(sem, "h_scan_ready")
        m_ready = per_batch(sem, "c_times_h_ready")
        m_summed = per_batch(sem, "c_times_h_summed")
        y0_ready = per_batch(sem, "y_lower_copied")
        ys_ready = per_batch(sem, "y_scan_copied")
        yback_done = per_batch(sem, "y_scan_transposed")
        fhid_done = per_batch(sem, "ffn_hidden_done")
        fhid_ready = per_batch(sem, "ffn_hidden_ready")
        fpred_done = per_batch(sem, "ffn_pred_done")
        fpred_ready = per_batch(sem, "ffn_pred_ready")
        fout_done = per_batch(sem, "ffn_out_done")
        o_ready = per_batch(sem, "o_ready")

        block = ctx.enter_context(nc.Block())

        LNF, LN_SCAN, LN_FFN, LN_OUT = 2 * LAYERS, 2 * LAYERS + 1, 2 * LAYERS + 2, 2 * LAYERS + 3

        def col(c, n=1, r=P):
            return cols[0:r, c:c + n]

        def parts(c):
            return P if c == 0 else W1

        NPAIR = NC_ // 2
        PIPE = 2
        LAYER = [("stats", 1.3), ("normed", 2.2), ("kq", 6), ("v", 1.5), ("k_back", 1.5), ("q_norm", 2.5), ("q_back", 2),
                 ("ctx", 3), ("ctx_outw", 2), ("att", 3)]
        FF = [("stats", 1.3), ("normed", 2.2), ("ff1", 5), ("ff2", 3)]
        path = [("conv", 0, 15)]
        for l in range(LAYERS):
            path += [(s, 2 * l, d) for s, d in LAYER] + [(s, 2 * l + 1, d) for s, d in FF]
        path += [("stats", 2 * LAYERS, 1.3), ("normed", 2 * LAYERS, 2.2), ("head", 0, 2),
                 ("h_stats", LN_SCAN, 2), ("h_normed", LN_SCAN, 4), ("scan_in", 0, 3), ("softplus", 0, 3)]
        path += [("scan", p, 2.6) for p in range(NPAIR + PIPE)]
        path += [("scan_out", 0, 3), ("h_stats", LN_FFN, 2), ("h_normed", LN_FFN, 4), ("ffn_hidden", 0, 2),
                 ("ffn_pred", 0, 2), ("ffn_out", 0, 4), ("out", 0, 5)]
        timed = []
        for b in range(NB):
            at = b * BEHIND
            for n, (stage, i, d) in enumerate(path):
                timed.append((at, n, b, stage, i))
                at += d
                if b == 0 and (stage, i) == ("conv", 0):
                    timed.append((at, n, b, "text", 0))
                if b == 0 and (stage, i) == ("kq", 0):
                    timed.append((at, n, b, "text_norm", 0))
        STAGES = [(stage, b, i) for _, _, b, stage, i in sorted(timed)]

        @block.sync
        def _(sp):
            sp.dma_start(ids_sb[:], ids).then_inc(s_ids, 16)
            for g in range(KT // KG):
                k = slice(g * KG, (g + 1) * KG)
                sp.dma_start(convw_sb[:, k, :], convw[:, k, :]).then_inc(s_patch0[g], 16)
                sp.dma_start(patch_sb[0][:, k, :], patches[0, :, k, :]).then_inc(s_patch0[g], 16)
                if g == 1:
                    sp.dma_start(cols[:], cols_d).then_inc(s_cols, 16)
            sp.dma_start(ident[:], ident_d).then_inc(s_ident, 16)
            sp.dma_start(rows[:, 0:ROW_BO], rows_d[0:ROW_BO].partition_broadcast(P)).then_inc(s_rows, 16)
            for l in range(LAYERS):
                sp.dma_start(qkv_sb[:, l], qkvw[:, l]).then_inc(s_qkv[l], 16)
                if l == 0:
                    for g in range(KT // KG):
                        k = slice(g * KG, (g + 1) * KG)
                        sp.dma_start(patch_sb[1][:, k, :], patches[1, :, k, :]).then_inc(s_patch1, 16)
                sp.dma_start(outw_sb[:, l], outw[:, l]).then_inc(s_outw[l], 16)
                sp.dma_start(ff1_sb[:, l], ff1w[:, l]).then_inc(s_outw[l], 16)
                sp.dma_start(ff2_sb[:, l], ff2w[:, l]).then_inc(s_outw[l], 16)
            sp.dma_start(rows[:, ROW_BO:NROWS], rows_d[ROW_BO:NROWS].partition_broadcast(P)).then_inc(s_rows2, 16)
            sp.dma_start(misc[:], misc_d).then_inc(s_misc, 16)
            sp.dma_start(sel[:], sel_d).then_inc(s_sel, 16)
            for b in range(NB):
                sp.wait_ge(o_ready[b], 1)
                sp.dma_start(out[b, 0:TOK, :].rearrange("(t p) w -> p t w", p=P), o[b][:, 0:NT, :]).then_inc(s_out, 16)
                sp.dma_start(out[b, TOK:L, :], o[b][0:S_TXT, NT, :]).then_inc(s_out, 16)
            sp.wait_ge(s_out, 2 * NB * 16)

        @block.gpsimd
        def _(pool):
            nc.gpsimd.memset(we[:, 0:1], 0.0)
            nc.gpsimd.memset(we[:, W + 1:W + 2], 0.0)
            nc.gpsimd.memset(pe_rows[:, 0:1], 0.0)
            nc.gpsimd.memset(pe_rows[:, W + 1:W + 2], 0.0).then_inc(s_edges, 1)
            pool.dma_start(tconst[:], tconst_d).then_inc(s_tconst, 16)
            for b in range(NB):
                pool.dma_start(pe_rows[b * S_TXT:(b + 1) * S_TXT, 1:W + 1], pos_emb[0:S_TXT, :]).then_inc(s_pos, 16)
            pool.wait_ge(s_ids, 16)
            pool.indirect_dma_start(out=we[:, 1:W + 1], out_offset=None, in_=word_emb,
                                    in_offset=bass.IndirectOffsetOnAxis(ap=ids_sb[:, 0:1], axis=0)).then_inc(s_word, 16)
            nc.gpsimd.memset(neghalf[:], -0.5).then_inc(s_fill, 1)
            pool.wait_ge(s_fill, 1)

            def inverse_root(b, i, tiles):
                pool.wait_ge(var_ready[b], i + 1)
                nc.gpsimd.tensor_tensor(rstd[b][:, 0:tiles], ve[b][:, 0:tiles], neghalf[:, 0:tiles],
                                        ALU.pow).then_inc(rstd_ready[b], 1)

            def add_bias(b, k, row):
                pool.wait_ge(x_ready[b], k)
                nc.gpsimd.tensor_tensor(xb[b][:], x[b][:],
                                        rows[:, row:row + D].unsqueeze(1).to_broadcast([P, NT, D]),
                                        ALU.add).then_inc(xb_ready[b], 1)

            pool.wait_ge(s_rows, 16)

            def sum_matrices():
                pool.wait_ge(inv_ready, 1)
                pool.wait_ge(s_ident, 16)
                pool.wait_ge(s_misc, 16)
                nc.gpsimd.tensor_tensor(sum0[:], ident[:].unsqueeze(1).to_broadcast([P, C0, P]),
                                        inv_a[:, 0:C0].unsqueeze(2).to_broadcast([P, C0, P]), ALU.mult)
                nc.gpsimd.tensor_tensor(sum1[:], misc[:, MI_FOLD:MI_FOLD + W1].unsqueeze(1).to_broadcast([P, C1, W1]),
                                        inv_a[:, C0:NC_].unsqueeze(2).to_broadcast([P, C1, W1]),
                                        ALU.mult).then_inc(sums_ready, 1)

            for stage, b, i in STAGES:
                if stage == "text_norm":
                    pool.wait_ge(s_txtvar, 1)
                    nc.gpsimd.tensor_tensor(trstd[:], tve[:], neghalf[0:S_TXT, 0:NB], ALU.pow).then_inc(s_txtrstd, 1)
                elif stage == "stats":
                    inverse_root(b, i, NT)
                    if i < 2 * LAYERS:
                        add_bias(b, i + 1, (ROW_FF2B if i % 2 else ROW_OUTB) + (i // 2) * D)
                elif stage == "kq" and b == 0 and i == 2:
                    sum_matrices()
                elif stage in ("h_stats", "out"):
                    inverse_root(b, i if stage == "h_stats" else LN_OUT, 3)
                elif stage == "scan" and i < NPAIR:
                    for c in (2 * i, 2 * i + 1):
                        pool.wait_ge(b_copied[b], c + 1)
                        if c >= RU:
                            pool.wait_ge(binc_ready[b], c - RU + 1)
                        nc.gpsimd.tensor_tensor(u[b][:, c % RU, :], bsp[b][:, c % 2, :],
                                                ht[b][:, 0 if c < C0 else 1, :], ALU.mult).then_inc(u_ready[b], 1)

        @block.vector
        def _(dve):
            steps = [0]

            def link(ins):
                steps[0] += 1
                ins.then_inc(dve_step, 1)
                dve.wait_ge(dve_step, steps[0])

            def norm_stats(b, i, src, width, tiles, eps):
                for t in range(tiles):
                    last = nc.vector.bn_stats(stats[b][0:ROWS[t], t, :], src[0:ROWS[t], t, 0:width])
                link(last)
                for t in range(tiles):
                    last = nc.vector.bn_aggr(mv[b][0:ROWS[t], t, :], stats[b][0:ROWS[t], t, :])
                link(last)
                nc.vector.tensor_scalar(ve[b][:, 0:tiles], mv[b][:, 0:tiles, 1], eps, None,
                                        ALU.add).then_inc(var_ready[b], 1)

            def normalise(b, i, dst, src, width, tiles):
                dve.wait_ge(rstd_ready[b], i + 1)
                for t in range(tiles):
                    r = ROWS[t]
                    last = nc.vector.tensor_scalar(dst[0:r, t, 0:width], src[0:r, t, 0:width], mv[b][0:r, t, 0:1],
                                                   rstd[b][0:r, t:t + 1], ALU.subtract, ALU.mult)
                return last

            for b in range(NB):
                nc.vector.memset(ctxt[b][:], 0.0)
                last = nc.vector.memset(mv[b][:], 1.0)
            link(last)
            dve.wait_ge(s_cols, 16)
            dve.wait_ge(s_tconst, 16)
            for i in range(3):
                shift = tconst[:, i * 2 * S_TXT:(i + 1) * 2 * S_TXT].unsqueeze(1).to_broadcast([2 * S_TXT, 6, 2 * S_TXT])
                taps = col(COL_CW + 6 * i, 6, 2 * S_TXT).unsqueeze(2).to_broadcast([2 * S_TXT, 6, 2 * S_TXT])
                link(nc.vector.tensor_tensor((band if i == 0 else band_t)[:], shift, taps, ALU.mult))
                if i:
                    ins = nc.vector.tensor_tensor(band[:], band[:], band_t[:], ALU.add)
                    if i == 1:
                        link(ins)
                    else:
                        ins.then_inc(s_band, 1)
            nc.vector.reciprocal(inv_a[:], col(COL_A, NC_)).then_inc(inv_ready, 1)
            nc.vector.tensor_tensor(pdelta[:], col(COL_PD, 2), col(COL_BD).to_broadcast([P, 2]),
                                    ALU.add).then_inc(pdelta_ready, 1)
            def text_norm():
                dve.wait_ge(s_txtgelu, 1)
                for b in range(NB):
                    last = nc.vector.bn_stats(tstats[:, b, :], txt[:, b, :])
                link(last)
                for b in range(NB):
                    last = nc.vector.bn_aggr(tmv[:, b, :], tstats[:, b, :])
                link(last)
                nc.vector.tensor_scalar(tve[:], tmv[:, :, 1], EPS_TXT, None, ALU.add).then_inc(s_txtvar, 1)
                dve.wait_ge(s_txtrstd, 1)
                for b in range(NB):
                    last = nc.vector.tensor_scalar(txt[:, b, :], txt[:, b, :], tmv[:, b, 0:1], trstd[:, b:b + 1],
                                                   ALU.subtract, ALU.mult)
                link(last)
                gains = rows[0:S_TXT, ROW_TG:ROW_TG + W].unsqueeze(1).to_broadcast([S_TXT, NB, W])
                dve.wait_ge(s_rows2, 16)
                link(nc.vector.tensor_tensor(txt[:], txt[:], gains, ALU.mult))
                for b in range(NB):
                    nc.vector.tensor_tensor(h[b][0:S_TXT, NT, :], txt[:, b, :], rows[0:S_TXT, ROW_TB:ROW_TB + W], ALU.add)

            def scan_pair(b, p):
                if p >= 2:
                    c = 2 * (p - 2)
                    dve.wait_ge(hs_ready[b], c + 2)
                    dve.wait_ge(c_spread[b], c + 2)
                    if c >= RM:
                        dve.wait_ge(m_summed[b], c - RM + 2)
                    nc.vector.tensor_tensor(m[b][:, c % RM:c % RM + 2, :], hs[b][:],
                                            pb[b][:].rearrange("p (c n) -> p c n", c=2)[:, :, 0:L],
                                            ALU.mult).then_inc(m_ready[b], 2)
                if 1 <= p < NPAIR + 1:
                    for c in (2 * p - 2, 2 * p - 1):
                        dve.wait_ge(u_ready[b], c + 1)
                        dve.wait_ge(abar_ready[b], c + 1)
                        if c >= RB:
                            dve.wait_ge(hs_ready[b], c - RB + 1)
                        nc.vector.scalar_tensor_tensor(binc[b][:, c % RB, :], abar[b][:, c % RA, :], col(COL_A + c),
                                                       u[b][:, c % RU, :], ALU.subtract,
                                                       ALU.mult).then_inc(binc_ready[b], 1)
                    for c in (2 * p - 2, 2 * p - 1):
                        dve.wait_ge(binc_ready[b], c + 1)
                        if c >= RH:
                            dve.wait_ge(m_ready[b], 2 * p - 2)
                        nc.vector.tensor_tensor_scan(hs[b][:, c % RH, :], abar[b][:, c % RA, :], binc[b][:, c % RB, :],
                                                     0.0, ALU.mult, ALU.add).then_inc(hs_ready[b], 1)

            for stage, b, i in STAGES:
                l = i // 2
                if stage == "text_norm":
                    text_norm()
                elif stage == "conv":
                    dve.wait_ge(conv_done[b], 1)
                    dve.wait_ge(s_rows, 16)
                    nc.vector.tensor_tensor(x[b][:], pa[b][:].rearrange("p (t w) -> p t w", t=NT)[:, :, 0:D],
                                            rows[:, ROW_CONVB:ROW_CONVB + D].unsqueeze(1).to_broadcast([P, NT, D]),
                                            ALU.add).then_inc(x_ready[b], 1)
                elif stage == "stats":
                    dve.wait_ge(x_ready[b], i + 1)
                    norm_stats(b, i, x[b], D, NT, EPS)
                elif stage == "normed":
                    normalise(b, i, xn[b], x[b], D, NT).then_inc(xn_ready[b], 1)
                elif stage == "kq":
                    dve.wait_ge(kt_done[b], l + 1)
                    nc.vector.tensor_reduce(kmax[b][:], pb[b][:].rearrange("p (j n) -> p j n", j=NJ), AX, ALU.max,
                                            negate=True).then_inc(kmax_ready[b], 1)
                    dve.wait_ge(q_done[b], l + 1)
                    link(nc.vector.tensor_reduce(qmax[b][:], pa[b][:].rearrange("p (h d) -> p h d", d=DH), AX, ALU.max))
                    nc.vector.tensor_tensor(q[b][:], pa[b][:].rearrange("p (h d) -> p h d", d=DH),
                                            qmax[b][:].unsqueeze(2).to_broadcast([P, NT * NH, DH]),
                                            ALU.subtract).then_inc(qsub_ready[b], 1)
                elif stage == "q_norm":
                    dve.wait_ge(eq_ready[b], l + 1)
                    link(nc.vector.tensor_reduce(qmax[b][:], q[b][:], AX, ALU.add))
                    link(nc.vector.reciprocal(qrec[b][:], qmax[b][:]))
                    nc.vector.tensor_tensor(q[b][:], q[b][:], qrec[b][:].unsqueeze(2).to_broadcast([P, NT * NH, DH]),
                                            ALU.mult).then_inc(qn_ready[b], 1)
                    dve.wait_ge(ek_ready[b], l + 1)
                    link(nc.vector.reciprocal(krec[b][:], ksum[b][:]))
                    nc.vector.tensor_scalar(krec[b][:], krec[b][:], DH ** -0.5, None, ALU.mult)
                elif stage == "ctx":
                    dve.wait_ge(ctx_done[b], l + 1)
                    r = slice(DH, 2 * DH)
                    nc.vector.tensor_copy(ctxt[b][r, :, r], pa[b][r, 0:BANK].rearrange("p (j d) -> p j d", j=NJ)[:, :, r]
                                          ).then_inc(ctx1_ready[b], 1)
                elif stage == "ctx_outw":
                    dve.wait_ge(cw_done[b], l + 1)
                    nc.vector.tensor_tensor(cw[b][:], pa[b][:, BANK:2 * BANK].rearrange("p (j d) -> p j d", j=NJ),
                                            krec[b][:].unsqueeze(2).to_broadcast([P, NJ, D]),
                                            ALU.mult).then_inc(cw_ready[b], 1)
                elif stage == "att":
                    dve.wait_ge(att_done[b], l + 1)
                    dve.wait_ge(xb_ready[b], 2 * l + 1)
                    nc.vector.tensor_tensor(x[b][:], pb[b][:, 0:NT * D].rearrange("p (t d) -> p t d", t=NT), xb[b][:],
                                            ALU.add).then_inc(x_ready[b], 1)
                elif stage == "ff2":
                    dve.wait_ge(ff2_done[b], l + 1)
                    dve.wait_ge(xb_ready[b], 2 * l + 2)
                    nc.vector.tensor_tensor(x[b][:], pa[b][:, 0:NT * D].rearrange("p (t d) -> p t d", t=NT), xb[b][:],
                                            ALU.add).then_inc(x_ready[b], 1)
                elif stage == "head":
                    dve.wait_ge(head_done[b], 1)
                    link(nc.vector.tensor_tensor(h[b][:, 0:NT, :],
                                                 pb[b][:].rearrange("p (t w) -> p t w", t=NT)[:, :, 0:W],
                                                 rows[:, ROW_HEADB:ROW_HEADB + W].unsqueeze(1).to_broadcast([P, NT, W]),
                                                 ALU.add))
                elif stage == "h_stats":
                    norm_stats(b, i, h[b], W, 3, EPS)
                elif stage == "h_normed":
                    last = normalise(b, i, hn[b], h[b], W, 3)
                    if i == LN_SCAN:
                        link(last)
                        nc.vector.tensor_copy(hn[b][:, 0:NT, W:2 * P], hn[b][:, 0:NT, P:W])
                        last = nc.vector.tensor_copy(hn[b][0:S_TXT, NT, W:2 * P], hn[b][0:S_TXT, NT, P:W])
                    last.then_inc(xn_ready[b], 1)
                elif stage == "scan_in":
                    K = 2 * N
                    dve.wait_ge(bc_ready[b], 2)
                    nc.vector.tensor_tensor(bcr[b][K:2 * K, :], bc[b][:], bc3[b][0:K, :], ALU.subtract)
                    link(nc.vector.tensor_tensor(bc3[b][K:2 * K, :], bc[b][:], bc3[b][0:K, :], ALU.subtract))
                    nc.vector.tensor_tensor(bc3[b][2 * K:3 * K, :], bcr[b][K:2 * K, :], bc3[b][K:2 * K, :],
                                            ALU.subtract).then_inc(bc3_ready[b], 1)
                    dve.wait_ge(zabs_ready[b], 1)
                    for c in range(2):
                        last = nc.vector.tensor_scalar(z[b][:, c, :], pb[b][:, BANK:BANK + L], pdelta[:, c:c + 1], 0.0,
                                                       ALU.add, ALU.max)
                    last.then_inc(z_read[b], 1)
                elif stage == "softplus":
                    dve.wait_ge(z_read[b], 1)
                    dve.wait_ge(lnz_ready[b], 1)
                    nc.vector.tensor_tensor(delta[b][:], z[b][:], ez[b][:], ALU.add).then_inc(delta_ready[b], 1)
                elif stage == "scan":
                    scan_pair(b, i)
                elif stage == "scan_out":
                    dve.wait_ge(yback_done[b], 1)
                    nc.vector.tensor_tensor(h[b][:, 0:NT, :], h[b][:, 0:NT, :],
                                            pb[b][:, 0:NT * W].rearrange("p (t w) -> p t w", t=NT), ALU.add)
                    link(nc.vector.tensor_tensor(h[b][0:S_TXT, NT, :], h[b][0:S_TXT, NT, :],
                                                 pb[b][0:S_TXT, BANK:BANK + W], ALU.add))
                elif stage == "ffn_out":
                    dve.wait_ge(s_rows2, 16)
                    dve.wait_ge(fout_done[b], 1)
                    bo = rows[:, ROW_BO:ROW_BO + W]
                    nc.vector.tensor_tensor(o[b][:, 0:NT, :], pb[b][:, 0:NT * W].rearrange("p (t w) -> p t w", t=NT),
                                            bo.unsqueeze(1).to_broadcast([P, NT, W]), ALU.add)
                    link(nc.vector.tensor_tensor(o[b][0:S_TXT, NT, :], pb[b][0:S_TXT, BANK:BANK + W], bo[0:S_TXT, :],
                                                 ALU.add))
                elif stage == "out":
                    norm_stats(b, LN_OUT, o[b], W, 3, EPS)
                    fb, fg = rows[:, ROW_FB:ROW_FB + W], rows[:, ROW_FG:ROW_FG + W]
                    nc.vector.tensor_tensor(h[b][:, 0:NT, :], h[b][:, 0:NT, :],
                                            fb.unsqueeze(1).to_broadcast([P, NT, W]), ALU.add)
                    nc.vector.tensor_tensor(h[b][0:S_TXT, NT, :], h[b][0:S_TXT, NT, :], fb[0:S_TXT, :], ALU.add)
                    link(normalise(b, LN_OUT, o[b], o[b], W, 3))
                    nc.vector.tensor_tensor(o[b][:, 0:NT, :], o[b][:, 0:NT, :],
                                            fg.unsqueeze(1).to_broadcast([P, NT, W]), ALU.mult)
                    link(nc.vector.tensor_tensor(o[b][0:S_TXT, NT, :], o[b][0:S_TXT, NT, :], fg[0:S_TXT, :], ALU.mult))
                    nc.vector.tensor_tensor(o[b][:, 0:NT, :], o[b][:, 0:NT, :], h[b][:, 0:NT, :], ALU.add)
                    nc.vector.tensor_tensor(o[b][0:S_TXT, NT, :], o[b][0:S_TXT, NT, :], h[b][0:S_TXT, NT, :],
                                            ALU.add).then_inc(o_ready[b], 1)

        @block.scalar
        def _(act):
            steps = [0]

            def link(ins):
                steps[0] += 1
                ins.then_inc(act_step, 1)
                act.wait_ge(act_step, steps[0])

            def affine(b, i, c):
                act.wait_ge(tr_done[b], i + 1)
                nc.scalar.activation(yt[b][:], pa[b][:, 0:TOK], ACT.Identity, bias=col(c + 1),
                                     scale=col(c)).then_inc(yt_ready[b], 1)

            loaded = [None]

            def tables(name):
                if loaded[0] != name:
                    nc.scalar.preload_act_table_set(name)
                    loaded[0] = name

            tables("gelu_and_others")
            act.wait_ge(s_cols, 16)

            for stage, b, i in STAGES:
                l = i // 2
                if stage == "text":
                    act.wait_ge(s_txtconv, 1)
                    for tb in range(NB):
                        last = nc.scalar.activation(txt[:, tb, :], pb[tb][0:S_TXT, 0:W], ACT.Gelu)
                    last.then_inc(s_txtgelu, 1)
                    tables("natural_log_exp_and_others")
                elif stage == "normed":
                    affine(b, i, COL_LNF if i == 2 * LAYERS else COL_LN + 2 * i)
                elif stage == "kq":
                    act.wait_ge(kmax_ready[b], l + 1)
                    tables("natural_log_exp_and_others")
                    for j in range(NJ):
                        last = nc.scalar.activation(ekt[b][:, j, :], pb[b][:, j * TOK:(j + 1) * TOK], ACT.Exp,
                                                    bias=kmax[b][:, j:j + 1], accum_out=ksum[b][:, j:j + 1])
                    last.then_inc(ek_ready[b], 1)
                    act.wait_ge(qsub_ready[b], l + 1)
                    nc.scalar.activation(q[b][:], q[b][:], ACT.Exp).then_inc(eq_ready[b], 1)
                elif stage == "v":
                    act.wait_ge(v_done[b], l + 1)
                    nc.scalar.activation(v[b][:].rearrange("p t w -> p (t w)"), pb[b][:],
                                         ACT.Copy).then_inc(v_ready[b], 1)
                elif stage == "k_back":
                    act.wait_ge(kn_done[b], l + 1)
                    nc.scalar.activation(kn[b][:].rearrange("p t w -> p (t w)"), pa[b][:],
                                         ACT.Copy).then_inc(kn_ready[b], 1)
                elif stage == "q_back":
                    act.wait_ge(qt_done[b], l + 1)
                    nc.scalar.activation(qt[b][:].rearrange("p j n -> p (j n)"), pb[b][:],
                                         ACT.Copy).then_inc(qt_ready[b], 1)
                elif stage == "ctx":
                    act.wait_ge(ctx_done[b], l + 1)
                    nc.scalar.activation(ctxt[b][0:DH, :, 0:DH],
                                         pa[b][0:DH, 0:BANK].rearrange("p (j d) -> p j d", j=NJ)[:, :, 0:DH],
                                         ACT.Copy).then_inc(ctx0_ready[b], 1)
                elif stage == "ff1":
                    act.wait_ge(ff1_done[b], l + 1)
                    tables("gelu_and_others")
                    for k in range(NM):
                        last = nc.scalar.activation(hid[b][:, k, :], pb[b][:, k * TOK:(k + 1) * TOK], ACT.Gelu,
                                                    bias=col(COL_FF1B + NM * l + k))
                    last.then_inc(gelu_done[b], 1)
                elif stage == "h_normed":
                    act.wait_ge(tr_done[b], i + 1)
                    if i == LN_SCAN:
                        nc.scalar.activation(ht[b][:], pa[b][:].rearrange("p (c n) -> p c n", c=2)[:, :, 0:L],
                                             ACT.Copy).then_inc(yt_ready[b], 1)
                    else:
                        nc.scalar.activation(ht[b][:, 0, :], pa[b][:, 0:L], ACT.Copy)
                        nc.scalar.activation(ht[b][0:W1, 1, :], pa[b][0:W1, BANK:BANK + L],
                                             ACT.Copy).then_inc(yt_ready[b], 1)
                elif stage == "scan_in":
                    act.wait_ge(bcd_done[b], 1)
                    nc.scalar.activation(bc[b][:], pb[b][0:2 * N, 0:L], ACT.Identity,
                                         bias=col(COL_BBC, 1, 2 * N)).then_inc(bc_ready[b], 1)
                    nc.scalar.activation(bc3[b][0:2 * N, :], pb[b][0:2 * N, 0:L], ACT.Identity,
                                         bias=col(COL_BBC, 1, 2 * N)).then_inc(bc_ready[b], 1)
                    act.wait_ge(pdelta_ready, 1)
                    for c in range(2):
                        last = nc.scalar.activation(ez[b][:, c, :], pb[b][:, BANK:BANK + L], ACT.Abs,
                                                    bias=pdelta[:, c:c + 1])
                    last.then_inc(zabs_ready[b], 1)
                    act.wait_ge(zabs_ready[b], 1)
                    tables("natural_log_exp_and_others")
                    link(nc.scalar.activation(ez[b][:], ez[b][:], ACT.Exp, scale=-1.0))
                    nc.scalar.activation(ez[b][:], ez[b][:], ACT.Ln, bias=1.0).then_inc(lnz_ready[b], 1)
                elif stage == "scan" and i < NPAIR:
                    if i == 0:
                        act.wait_ge(delta_ready[b], 1)
                    tables("natural_log_exp_and_others")
                    for c in (2 * i, 2 * i + 1):
                        if c >= RA:
                            act.wait_ge(hs_ready[b], c - RA + 1)
                        nc.scalar.activation(abar[b][:, c % RA, :], delta[b][:, 0 if c < C0 else 1, :], ACT.Exp,
                                             scale=col(COL_A + c)).then_inc(abar_ready[b], 1)
                        act.wait_ge(b_spread[b], c + 1)
                        if c >= 2:
                            act.wait_ge(u_ready[b], c - 1)
                        nc.scalar.activation(bsp[b][:, c % 2, :], pa[b][:, BANK:BANK + L],
                                             ACT.Copy).then_inc(b_copied[b], 1)
                        if c == C0 + 4:
                            act.wait_ge(m_summed[b], C0)
                            nc.scalar.activation(ys[b][:, 0, :], pa[b][:, 0:L], ACT.Copy).then_inc(y0_ready[b], 1)
                elif stage == "scan_out":
                    act.wait_ge(m_summed[b], NC_)
                    nc.scalar.activation(ys[b][0:W1, 1, :], pa[b][0:W1, 0:L],
                                         ACT.Copy).then_inc(ys_ready[b], 1)
                elif stage == "ffn_hidden":
                    act.wait_ge(fhid_done[b], 1)
                    nc.scalar.activation(fhid[b][:], pb[b][:, 0:L], ACT.Relu,
                                         bias=col(COL_B1)).then_inc(fhid_ready[b], 1)
                elif stage == "ffn_pred":
                    act.wait_ge(fpred_done[b], 1)
                    nc.scalar.activation(fpred[b][:, 0, :], pa[b][:, 0:L], ACT.Identity, bias=col(COL_B2))
                    nc.scalar.activation(fpred[b][0:W1, 1, :], pa[b][0:W1, BANK:BANK + L], ACT.Identity,
                                         bias=col(COL_B2 + 1, 1, W1)).then_inc(fpred_ready[b], 1)

        @block.tensor
        def _(pe):
            def mm(dst, lhs_t, rhs, first=True, last=True):
                return nc.tensor.matmul(dst, lhs_t, rhs, start=first, stop=last)

            def to_features(b, i):
                pe.wait_ge(xn_ready[b], i + 1)
                for t in range(NT):
                    last = nc.tensor.transpose(pa[b][:, t * P:(t + 1) * P], xn[b][:, t, :], ident[:])
                last.then_inc(tr_done[b], 1)

            def h_to_features(b, i, second):
                pe.wait_ge(xn_ready[b], i + 1)
                for t in range(3):
                    r = ROWS[t]
                    nc.tensor.transpose(pa[b][:, t * P:t * P + r], hn[b][0:r, t, 0:P], ident[0:r, 0:r])
                    last = nc.tensor.transpose(pa[b][0:second, BANK + t * P:BANK + t * P + r],
                                               hn[b][0:r, t, P:P + second], ident[0:r, 0:r])
                last.then_inc(tr_done[b], 1)

            def spread_b(b, c):
                if c:
                    pe.wait_ge(b_copied[b], c)
                mm(pa[b][:, BANK:BANK + L], sel[:, 2 * c, :], bc3[b][:]).then_inc(b_spread[b], 1)

            def spread_c(b, p):
                if p:
                    pe.wait_ge(m_ready[b], 2 * p)
                for e in range(2):
                    last = mm(pb[b][:, e * BANK:e * BANK + L], sel[:, 2 * (2 * p + e) + 1, :], bc3[b][:])
                last.then_inc(c_spread[b], 2)

            def sum_m(b, c):
                pe.wait_ge(m_ready[b], c + 1)
                src = m[b][:, c % RM, :]
                if c < C0:
                    mm(pa[b][:, 0:L], sum0[:, c, :], src, c == 0, c == C0 - 1).then_inc(m_summed[b], 1)
                else:
                    if c == C0:
                        pe.wait_ge(y0_ready[b], 1)
                    mm(pa[b][0:W1, 0:L], sum1[:, c - C0, :], src, c == C0, c == NC_ - 1).then_inc(m_summed[b], 1)

            for stage, b, i in STAGES:
                l = i // 2
                if stage == "text":
                    pe.wait_ge(s_band, 1)
                    pe.wait_ge(s_edges, 1)
                    pe.wait_ge(s_pos, 16 * NB)
                    pe.wait_ge(s_word, 16)
                    for tb in range(NB):
                        for k in range(6):
                            src = we if k < 3 else pe_rows
                            last = mm(pb[tb][0:S_TXT, 0:W], band[:, k, tb * S_TXT:(tb + 1) * S_TXT],
                                      src[:, k % 3:k % 3 + W], k == 0, k == 5)
                    last.then_inc(s_txtconv, 1)
                elif stage == "conv":
                    for g in range(KT // KG):
                        if b == 0:
                            pe.wait_ge(s_patch0[g], 2 * 16)
                        elif g == 0:
                            pe.wait_ge(s_patch1, 16 * KT // KG)
                        for k in range(g * KG, (g + 1) * KG):
                            for t in range(NT):
                                last = mm(pa[b][:, t * BANK:t * BANK + D], patch_sb[b][:, k, t * P:(t + 1) * P],
                                          convw_sb[:, k, :], k == 0, k == KT - 1)
                    last.then_inc(conv_done[b], 1)
                elif stage == "normed":
                    if i == 0:
                        pe.wait_ge(s_ident, 16)
                    to_features(b, i)
                elif stage == "kq":
                    pe.wait_ge(yt_ready[b], 2 * l + 1)
                    pe.wait_ge(s_qkv[l], 16)
                    if l == 0:
                        pe.wait_ge(s_txtgelu, 1)
                    for j in range(NJ):
                        last = mm(pb[b][:, j * TOK:(j + 1) * TOK], qkv_sb[:, l, INNER + j * P:INNER + (j + 1) * P],
                                  yt[b][:])
                    last.then_inc(kt_done[b], 1)
                    for t in range(NT):
                        last = mm(pa[b][:, t * BANK:(t + 1) * BANK], yt[b][:, t * P:(t + 1) * P], qkv_sb[:, l, 0:INNER])
                    last.then_inc(q_done[b], 1)
                elif stage == "v":
                    pe.wait_ge(ek_ready[b], l + 1)
                    for t in range(NT):
                        last = mm(pb[b][:, t * BANK:(t + 1) * BANK], yt[b][:, t * P:(t + 1) * P],
                                  qkv_sb[:, l, 2 * INNER:3 * INNER])
                    last.then_inc(v_done[b], 1)
                elif stage == "k_back":
                    pe.wait_ge(qsub_ready[b], l + 1)
                    for t in range(NT):
                        for j in range(NJ):
                            last = nc.tensor.transpose(pa[b][:, t * BANK + j * P:t * BANK + (j + 1) * P],
                                                       ekt[b][:, j, t * P:(t + 1) * P], ident[:])
                    last.then_inc(kn_done[b], 1)
                elif stage == "q_back":
                    pe.wait_ge(qn_ready[b], l + 1)
                    pe.wait_ge(v_ready[b], l + 1)
                    qv = q[b][:].rearrange("p (t e) d -> p t (e d)", t=NT)
                    for j in range(NJ):
                        for t in range(NT):
                            last = nc.tensor.transpose(pb[b][:, j * TOK + t * P:j * TOK + (t + 1) * P],
                                                       qv[:, t, j * P:(j + 1) * P], ident[:])
                    last.then_inc(qt_done[b], 1)
                elif stage == "ctx":
                    pe.wait_ge(kn_ready[b], l + 1)
                    pe.wait_ge(v_ready[b], l + 1)
                    for j in range(NJ):
                        for t in range(NT):
                            last = mm(pa[b][:, j * P:(j + 1) * P], v[b][:, t, j * P:(j + 1) * P],
                                      kn[b][:, t, j * P:(j + 1) * P], t == 0, t == NT - 1)
                    last.then_inc(ctx_done[b], 1)
                elif stage == "ctx_outw":
                    pe.wait_ge(ctx0_ready[b], l + 1)
                    pe.wait_ge(ctx1_ready[b], l + 1)
                    pe.wait_ge(s_outw[l], 3 * 16)
                    for j in range(NJ):
                        last = mm(pa[b][:, BANK + j * D:BANK + (j + 1) * D], ctxt[b][:, j, :], outw_sb[:, l, j, :])
                    last.then_inc(cw_done[b], 1)
                elif stage == "att":
                    pe.wait_ge(cw_ready[b], l + 1)
                    pe.wait_ge(qt_ready[b], l + 1)
                    for t in range(NT):
                        for j in range(NJ):
                            last = mm(pb[b][:, t * D:(t + 1) * D], qt[b][:, j, t * P:(t + 1) * P], cw[b][:, j, :],
                                      j == 0, j == NJ - 1)
                    last.then_inc(att_done[b], 1)
                elif stage == "ff1":
                    pe.wait_ge(yt_ready[b], 2 * l + 2)
                    for k in range(NM):
                        last = mm(pb[b][:, k * TOK:(k + 1) * TOK], ff1_sb[:, l, k * P:(k + 1) * P], yt[b][:])
                    last.then_inc(ff1_done[b], 1)
                elif stage == "ff2":
                    pe.wait_ge(gelu_done[b], l + 1)
                    for t in range(NT):
                        for k in range(NM):
                            last = mm(pa[b][:, t * D:(t + 1) * D], hid[b][:, k, t * P:(t + 1) * P], ff2_sb[:, l, k, :],
                                      k == 0, k == NM - 1)
                    last.then_inc(ff2_done[b], 1)
                elif stage == "head":
                    pe.wait_ge(yt_ready[b], LNF + 1)
                    pe.wait_ge(s_misc, 16)
                    for t in range(NT):
                        last = mm(pb[b][:, t * BANK:t * BANK + W], yt[b][:, t * P:(t + 1) * P],
                                  misc[:, MI_HEAD:MI_HEAD + W])
                    last.then_inc(head_done[b], 1)
                elif stage == "h_normed":
                    h_to_features(b, i, P if i == LN_SCAN else W1)
                elif stage == "scan_in":
                    pe.wait_ge(yt_ready[b], LN_SCAN + 1)
                    for c in range(2):
                        r = parts(c)
                        mm(pb[b][0:2 * N, 0:L], misc[0:r, MI_BC + 2 * N * c:MI_BC + 2 * N * (c + 1)], ht[b][0:r, c, :],
                           c == 0, c == 1)
                    for c in range(2):
                        r = parts(c)
                        last = mm(pb[b][:, BANK:BANK + L], misc[0:r, MI_WD + P * c:MI_WD + P * (c + 1)],
                                  ht[b][0:r, c, :], c == 0, c == 1)
                    last.then_inc(bcd_done[b], 1)
                elif stage == "scan":
                    if i == 0:
                        pe.wait_ge(bc3_ready[b], 1)
                        pe.wait_ge(s_sel, 16)
                        pe.wait_ge(sums_ready, 1)
                    if i < NPAIR:
                        spread_b(b, 2 * i)
                    if i == 0:
                        pe.wait_ge(z_read[b], 1)
                        pe.wait_ge(lnz_ready[b], 1)
                        spread_c(b, 0)
                    elif 2 <= i < NPAIR + 1:
                        spread_c(b, i - 1)
                    if i < NPAIR:
                        spread_b(b, 2 * i + 1)
                    if i >= 3:
                        sum_m(b, 2 * (i - 3))
                        sum_m(b, 2 * (i - 3) + 1)
                    if i == NPAIR + PIPE - 1:
                        sum_m(b, NC_ - 2)
                        sum_m(b, NC_ - 1)
                elif stage == "scan_out":
                    pe.wait_ge(ys_ready[b], 1)
                    for t in range(3):
                        r = ROWS[t]
                        base = t * W if t < NT else BANK
                        nc.tensor.transpose(pb[b][0:r, base:base + P], ys[b][:, 0, t * P:t * P + r], ident[:])
                        last = nc.tensor.transpose(pb[b][0:r, base + P:base + W], ys[b][0:W1, 1, t * P:t * P + r],
                                                   ident[0:W1, 0:W1])
                    last.then_inc(yback_done[b], 1)
                elif stage == "ffn_hidden":
                    pe.wait_ge(yt_ready[b], LN_FFN + 1)
                    for c in range(2):
                        r = parts(c)
                        last = mm(pb[b][:, 0:L], misc[0:r, MI_W1 + FFI * c:MI_W1 + FFI * (c + 1)], ht[b][0:r, c, :],
                                  c == 0, c == 1)
                    last.then_inc(fhid_done[b], 1)
                elif stage == "ffn_pred":
                    pe.wait_ge(fhid_ready[b], 1)
                    mm(pa[b][:, 0:L], misc[:, MI_W2:MI_W2 + P], fhid[b][:])
                    mm(pa[b][0:W1, BANK:BANK + L], misc[:, MI_W2 + P:MI_W2 + W], fhid[b][:]).then_inc(fpred_done[b], 1)
                elif stage == "ffn_out":
                    pe.wait_ge(fpred_ready[b], 1)
                    for t in range(3):
                        r = ROWS[t]
                        base = t * W if t < NT else BANK
                        for c in range(2):
                            k = parts(c)
                            last = mm(pb[b][0:r, base:base + W], fpred[b][0:k, c, t * P:t * P + r],
                                      misc[0:k, MI_WO + W * c:MI_WO + W * (c + 1)], c == 0, c == 1)
                    last.then_inc(fout_done[b], 1)


def kernel(**inputs):
    import concourse.bacc as bacc
    import ml_dtypes
    from concourse.bass_utils import run_bass_kernel_spmd

    a = {k: np.asarray(x) for k, x in inputs.items()}
    f32 = np.float32

    def two_parts(w):
        second = np.zeros((P, w.shape[1]), f32)
        second[:W1] = w[P:]
        return np.concatenate([w[:P], second], axis=1)

    def column(v, rows=P):
        c = np.zeros((P, 1), f32)
        c[:rows, 0] = v
        return c

    x = a["x"].reshape(NB, 32, 16, 8, 16, 8)
    patches = x.transpose(0, 1, 3, 5, 2, 4).reshape(NB, KT, P, TOK).transpose(0, 2, 1, 3)
    convw = a["L0_tok_conv_w"].reshape(D, KT, P).transpose(2, 1, 0)
    qkvw = a["L0_tok_qkv_w"].transpose(1, 0, 2)
    outw = a["L0_tok_out_w"].reshape(LAYERS, NJ, P, D).transpose(2, 0, 1, 3)
    ff1w = a["L0_tok_ff1_w"].transpose(1, 0, 2)
    ff2w = a["L0_tok_ff2_w"].reshape(LAYERS, NM, P, D).transpose(2, 0, 1, 3)

    cols = []
    for l in range(LAYERS):
        for n in ("ln1_g", "ln1_b", "ln2_g", "ln2_b"):
            cols.append(column(a["L0_tok_" + n][l]))
    cols += [column(a["L0_tok_lnf_g"]), column(a["L0_tok_lnf_b"])]
    cols.append(a["L0_tok_ff1_b"].reshape(LAYERS * NM, P).T)
    cols.append(column(np.concatenate([a["L0_attn_b_B"], a["L0_attn_b_C"]]), 2 * N))
    cols.append(column(a["L0_ffn_b1"]))
    cols += [column(a["L0_ffn_b2"][:P]), column(a["L0_ffn_b2"][P:], W1)]
    pd = a["L0_attn_p_Delta"]
    cols += [column(pd[:P]), column(np.tile(pd[P:], 2))]
    cols.append(np.broadcast_to(a["L0_attn_b_D"].reshape(1, 1), (P, 1)))
    aa = a["L0_attn_A"]
    cols.append(aa[:P])
    cols.append(np.concatenate([aa[P:, :C1], aa[P:, C1:]], axis=0))
    taps = a["L0_txt_conv_w"][0].transpose(1, 0, 2).reshape(1, 18)
    cols.append(np.broadcast_to(taps, (P, 18)))
    cols = np.ascontiguousarray(np.concatenate(cols, axis=1))
    assert cols.shape == (P, NCOLS)

    rows = np.concatenate([
        a["L0_tok_conv_b"], a["L0_tok_out_b"].ravel(), a["L0_tok_ff2_b"].ravel(), a["L0_tok_head_b"],
        a["L0_ffn_bo"], a["L0_ffn_gamma"], a["L0_ffn_beta"], a["L0_txt_ln_gamma"], a["L0_txt_ln_beta"]])
    assert rows.shape == (NROWS,)

    w_bc = np.concatenate([a["L0_attn_W_B"], a["L0_attn_W_C"]], axis=1)
    fold = np.zeros((P, W1), f32)
    fold[np.arange(P), np.arange(P) % W1] = 1.0
    misc = np.concatenate([
        a["L0_tok_head_w"], two_parts(w_bc), two_parts(np.broadcast_to(a["L0_attn_W_D"], (W, P))),
        two_parts(a["L0_ffn_W1"].T), a["L0_ffn_W2"].T, two_parts(a["L0_ffn_Wo"].T), fold], axis=1)
    assert misc.shape == (P, NMISC)

    shifts = np.zeros((2 * S_TXT, 3, 2 * S_TXT), f32)
    for i in range(3):
        for s in range(2 * S_TXT):
            if 0 <= s % S_TXT + i - 1 < S_TXT:
                shifts[s + i - 1, i, s] = 1.0
    sel = np.zeros((3, 2 * N, NC_, 2, P), f32)
    for c in range(NC_):
        states = [c, c] if c < C0 else [c - C0, c - C0 + C1]
        for half, n in enumerate(states):
            cut = slice(half * W1, (half + 1) * W1)
            sel[:, n, c, 0, cut] = 1.0
            sel[:, N + n, c, 1, cut] = 1.0
    arrays = {
        "ids": a["x_txt"].astype(np.int32).reshape(2 * S_TXT, 1),
        "patches": patches, "convw": convw, "qkvw": qkvw, "outw": outw, "ff1w": ff1w, "ff2w": ff2w,
        "cols": cols, "rows": rows, "misc": misc, "ident": np.eye(P, dtype=f32),
        "tconst": shifts.reshape(2 * S_TXT, NTC),
        "sel": sel.reshape(3 * 2 * N, 2 * NC_, P).astype(ml_dtypes.bfloat16),
        "word_emb": a["L0_txt_word_emb"], "pos_emb": a["L0_txt_pos_emb"],
    }
    nc = bacc.Bacc("TRN2", target_bir_lowering=False, num_devices=1)
    laid, args = {}, []
    for name, arr in arrays.items():
        arr = np.ascontiguousarray(arr)
        laid[f"in_{name}"] = arr
        args.append(nc.dram_tensor(f"in_{name}", arr.shape, mybir.dt.from_np(arr.dtype), kind="ExternalInput").ap())
    args.append(nc.dram_tensor("out", (NB, L, W), F32, kind="ExternalOutput").ap())
    build(nc, *args)
    r = run_bass_kernel_spmd(nc, [laid], core_ids=[0])
    return r.results[0]["out"]
```

```python
from contextlib import ExitStack

import numpy as np

import concourse.bass as bass
from concourse import mybir

F32 = mybir.dt.float32
BF16 = mybir.dt.bfloat16
I32 = mybir.dt.int32
ALU = mybir.AluOpType
ACT = mybir.ActivationFunctionType
AX = mybir.AxisListType.X

P = 128
NB = 2
D = 128
NT = 2
TOK = NT * P
KT = 16
GROUPS = [slice(0, 2), slice(2, 6), slice(6, 10), slice(10, KT)]
NG = len(GROUPS)
LAYERS = 2
NH, DH = 8, 64
INNER = NH * DH
NJ = INNER // P
M = 512
NM = M // P
W = 192
W1 = W - P
S_TXT = 32
L = TOK + S_TXT
ROWS = [P, P, S_TXT]
N = 16
C0, C1 = N, N // 2
NC_ = C0 + C1
BANK = 512
FFI = 128

PLAN = {
    "pe": "0000010101100001001101111000011011110100010111010000100100110101001110111010010001110101110001100100"
        "0110110011010100100111010010110100100111100101011101010111110000010100110100010110110001111000011001"
        "110000011110001111001011",
    "dve": "1010100000011010001101101000100101110011100101100100010110010101001001111111000001101010110100011001"
        "0100001101011101011100101010100101101010111010101010101001101010101010100110101001010010100111100101"
        "0110011",
    "act": "0000100011000101101111100100111000100000010101111110110010011011000100010010010010111010011100110011"
        "111000101100101011010101101110110100101101000010110010110011001110100011010011",
    "pool": "00100101001010100000111011011010011001011011010011100001011001011010011",
}

COL_LN = 0
COL_LNF = COL_LN + 4 * LAYERS
COL_FF1B = COL_LNF + 2
COL_BBC = COL_FF1B + NM * LAYERS
COL_B1 = COL_BBC + 1
COL_B2 = COL_B1 + 1
COL_PD = COL_B2 + 2
COL_BD = COL_PD + 2
COL_A = COL_BD + 1
COL_CW = COL_A + NC_
NCOLS = COL_CW + 18
ROW_CONVB = 0
ROW_OUTB = ROW_CONVB + D
ROW_FF2B = ROW_OUTB + LAYERS * D
ROW_HEADB = ROW_FF2B + LAYERS * D
ROW_BO = ROW_HEADB + W
ROW_FG = ROW_BO + W
ROW_FB = ROW_FG + W
ROW_TG = ROW_FB + W
ROW_TB = ROW_TG + W
NROWS = ROW_TB + W
MI_HEAD = 0
MI_BC = MI_HEAD + W
MI_WD = MI_BC + 2 * 2 * N
MI_W1 = MI_WD + 2 * P
MI_W2 = MI_W1 + 2 * FFI
MI_WO = MI_W2 + 2 * FFI
MI_FOLD = MI_WO + 2 * W
NMISC = MI_FOLD + W1
TC_SHIFT = 0
NTC = 3 * 2 * S_TXT

EPS = 1e-5
EPS_TXT = 1e-12


def build(nc, ids, patches, convw, qkvw, outw, ff1w, ff2w, cols_d, rows_d, misc_d, ident_d, tconst_d,
          sel_d, word_emb, pos_emb, out):
    ctx = ExitStack()
    with ctx:
        def sb(name, shape, dt=F32):
            return ctx.enter_context(nc.sbuf_tensor(name, shape, dt))

        def sem(name):
            return ctx.enter_context(nc.semaphore(name))

        def per_batch(make, name):
            return [make(f"{name}_{b}") for b in range(NB)]

        patch_sb = [sb(f"patch_{b}", [P, KT, TOK]) for b in range(NB)]
        convw_sb = sb("convw", [P, KT, D])
        qkv_sb = sb("qkvw", [P, LAYERS, 3 * INNER])
        outw_sb = sb("outw", [P, LAYERS, NJ, D])
        ff1_sb = sb("ff1w", [P, LAYERS, M])
        ff2_sb = sb("ff2w", [P, LAYERS, NM, D])
        cols = sb("cols", [P, NCOLS])
        rows = sb("rows", [P, NROWS])
        misc = sb("misc", [P, NMISC])
        ident = sb("ident", [P, P])
        tconst = sb("tconst", [2 * S_TXT, NTC])
        sel = sb("sel", [3 * 2 * N, 2 * C0 + 2 * C1, P], BF16)
        ids_sb = sb("ids", [2 * S_TXT, 1], I32)
        neghalf = sb("neghalf", [P, 4])
        inv_a = sb("inv_a", [P, NC_])
        sum0 = sb("sum_lower", [P, C0, P])
        sum1 = sb("sum_upper", [P, C1, W1])
        pdelta = sb("pdelta", [P, 2])
        we = sb("word_rows", [2 * S_TXT, W + 2])
        pe_rows = sb("pos_rows", [2 * S_TXT, W + 2])
        band = sb("band", [2 * S_TXT, 6, 2 * S_TXT])
        band_t = sb("band_term", [2 * S_TXT, 6, 2 * S_TXT])
        txt = sb("txt", [NB * S_TXT, W])
        tstats, tmv = sb("txt_stats", [NB * S_TXT, 6]), sb("txt_mean_var", [NB * S_TXT, 2])
        tve, trstd = sb("txt_var_eps", [NB * S_TXT, 1]), sb("txt_rstd", [NB * S_TXT, 1])
        x = per_batch(lambda n: sb(n, [P, NT, D]), "x")
        xb = per_batch(lambda n: sb(n, [P, NT, D]), "x_plus_bias")
        xn = per_batch(lambda n: sb(n, [P, NT, D]), "x_normed")
        yt = per_batch(lambda n: sb(n, [P, TOK]), "y_t")
        stats = per_batch(lambda n: sb(n, [P, 3, 6]), "stats")
        mv = per_batch(lambda n: sb(n, [P, 3, 2]), "mean_var")
        ve = per_batch(lambda n: sb(n, [P, 3]), "var_eps")
        rstd = per_batch(lambda n: sb(n, [P, 3]), "rstd")
        kmax = per_batch(lambda n: sb(n, [P, NJ]), "neg_kmax")
        ksum = per_batch(lambda n: sb(n, [P, NJ]), "ksum")
        krec = per_batch(lambda n: sb(n, [P, NJ]), "krec")
        ekt = per_batch(lambda n: sb(n, [P, NJ, TOK]), "exp_k_t")
        kn = per_batch(lambda n: sb(n, [P, NT, INNER]), "exp_k")
        v = per_batch(lambda n: sb(n, [P, NT, INNER]), "v")
        qmax = per_batch(lambda n: sb(n, [P, NT * NH]), "qmax")
        qrec = per_batch(lambda n: sb(n, [P, NT * NH]), "qrec")
        q = per_batch(lambda n: sb(n, [P, NT * NH, DH]), "q")
        qt = per_batch(lambda n: sb(n, [P, NJ, TOK]), "q_t")
        ctxt = per_batch(lambda n: sb(n, [P, NJ, P]), "ctx_t")
        cw = per_batch(lambda n: sb(n, [P, NJ, D]), "ctx_outw")
        hid = ekt
        h = per_batch(lambda n: sb(n, [P, 3, W]), "h")
        hn = per_batch(lambda n: sb(n, [P, 3, 2 * P]), "h_normed")
        ht = per_batch(lambda n: sb(n, [P, 2, L]), "h_t")
        bc = per_batch(lambda n: sb(n, [2 * N, L]), "bc")
        bcr = per_batch(lambda n: sb(n, [4 * N, L]), "bc_rest")
        bc3 = per_batch(lambda n: sb(n, [3 * 2 * N, L], BF16), "bc_parts")
        z = per_batch(lambda n: sb(n, [P, 2, L]), "z_above_zero")
        ez = per_batch(lambda n: sb(n, [P, 2, L]), "exp_z")
        delta = per_batch(lambda n: sb(n, [P, 2, L]), "delta")
        ys = ez
        fhid = per_batch(lambda n: sb(n, [P, L]), "ffn_hidden")
        hb = [z[b][:].rearrange("p c n -> p (c n)").rearrange("p (t w) -> p t w", w=W) for b in range(NB)]
        w2o = sb("ffn_w2_wo", [P, W])
        bo2 = sb("ffn_b2_wo_plus_bo", [P, W])
        o = per_batch(lambda n: sb(n, [P, 3, W]), "o")
        RA, RB, RH, RM, RU, RS = 6, 2, 2, 4, 3, 3
        flat = [patch_sb[b][:].rearrange("p k n -> p (k n)") for b in range(NB)]
        flat_w = convw_sb[:].rearrange("p k n -> p (k n)")

        def ring(src, first, n, width=L):
            return src[:, first:first + n * width].rearrange("p (r n) -> p r n", r=n)

        LS = L + 1
        abar = [ring(flat[b], 0, RA, LS) for b in range(NB)]
        binc = [ring(flat[b], RA * LS, RB, LS) for b in range(NB)]
        hs = [ring(flat[b], (RA + RB) * LS, RH, LS) for b in range(NB)]
        m = [ring(flat[b], (RA + RB + RH) * LS, RM) for b in range(NB)]

        def through(slots, c):
            return slots[:, c:c + 2, :].rearrange("p r n -> p (r n)")[:, 1:]

        u = [ring(flat_w, b * RU * L, RU) for b in range(NB)]
        bsp = [ring(kn[b][:].rearrange("p t w -> p (t w)"), 0, RS) for b in range(NB)]

        pa = [ctx.enter_context(nc.psum_tensor(f"pa_{b}", [P, 2 * BANK], F32)) for b in range(NB)]
        pb = [ctx.enter_context(nc.psum_tensor(f"pb_{b}", [P, 2 * BANK], F32)) for b in range(NB)]

        s_ids = sem("ids_loaded")
        s_patch0 = [sem(f"patch_0_and_convw_loaded_{g}") for g in range(NG)]
        s_patch1 = [sem(f"patch_1_loaded_{g}") for g in range(NG)]
        s_cols, s_rows, s_rows2 = sem("cols_loaded"), sem("rows_loaded"), sem("late_rows_loaded")
        s_misc, s_ident = sem("misc_loaded"), sem("ident_loaded")
        s_tconst, s_pos, s_word, s_sel = sem("tconst_loaded"), sem("pos_loaded"), sem("words_gathered"), sem("sel_loaded")
        s_qkv, s_outw = ([sem(f"{n}_loaded_{l}") for l in range(LAYERS)]
                                       for n in ("qkvw", "outw_ff1w_ff2w"))
        s_out = sem("out_written")
        s_fill, s_edges = sem("pool_fills_done"), sem("edges_zeroed")
        s_band, s_txtconv, s_txtgelu = sem("band_ready"), sem("txt_conv_done"), sem("txt_gelu_done")
        s_txtvar, s_txtrstd = sem("txt_var_ready"), sem("txt_rstd_ready")
        dve_step = sem("dve_step")
        act_step = sem("act_step")
        conv_done = per_batch(sem, "conv_done")
        x_ready = per_batch(sem, "x_ready")
        xb_ready = per_batch(sem, "x_plus_bias_ready")
        var_ready = per_batch(sem, "var_ready")
        rstd_ready = per_batch(sem, "rstd_ready")
        xn_ready = per_batch(sem, "normed_ready")
        tr_done = per_batch(sem, "normed_transposed")
        yt_ready = per_batch(sem, "normed_t_ready")
        kt_done = per_batch(sem, "k_done")
        q_done = per_batch(sem, "q_done")
        v_done = per_batch(sem, "v_done")
        kmax_ready = per_batch(sem, "kmax_ready")
        ek_ready = per_batch(sem, "exp_k_ready")
        qsub_ready = per_batch(sem, "q_shifted")
        eq_ready = per_batch(sem, "exp_q_ready")
        qn_ready = per_batch(sem, "q_normed")
        v_ready = per_batch(sem, "v_copied")
        kn_done = per_batch(sem, "exp_k_transposed")
        kn_ready = per_batch(sem, "exp_k_copied")
        qt_done = per_batch(sem, "q_transposed")
        qt0_ready = per_batch(sem, "q_t_copied_first_half")
        qt_ready = per_batch(sem, "q_t_copied_second_half")
        ctx_done = per_batch(sem, "ctx_done")
        ctx0_ready = per_batch(sem, "ctx_even_heads_copied")
        ctx1_ready = per_batch(sem, "ctx_odd_heads_copied")
        cw_done = per_batch(sem, "ctx_outw_done")
        cw_ready = per_batch(sem, "ctx_outw_copied")
        att_done = per_batch(sem, "att_done")
        ff1_done = per_batch(sem, "ff1_done")
        gelu_done = per_batch(sem, "gelu_done")
        ff2_done = per_batch(sem, "ff2_done")
        head_done = per_batch(sem, "head_done")
        bc_done = per_batch(sem, "bc_product_done")
        z_done = per_batch(sem, "z_product_done")
        bc_ready = per_batch(sem, "bc_copied")
        z_read = per_batch(sem, "z_read")
        zabs_ready = per_batch(sem, "abs_z_ready")
        sums_ready = sem("sum_matrices_ready")
        inv_ready = sem("inv_a_ready")
        pdelta_ready = sem("pdelta_ready")
        bc1_ready = per_batch(sem, "bc_first_part_ready")
        lnz_ready = per_batch(sem, "ln_exp_ready")
        bc3_ready = per_batch(sem, "bc_parts_ready")
        delta_ready = per_batch(sem, "delta_ready")
        b_spread = per_batch(sem, "b_spread")
        b_copied = per_batch(sem, "b_copied")
        c_spread = per_batch(sem, "c_spread")
        abar_ready = per_batch(sem, "a_bar_ready")
        u_ready = per_batch(sem, "u_ready")
        binc_ready = per_batch(sem, "b_inc_ready")
        hs_ready = per_batch(sem, "h_scan_ready")
        m_ready = per_batch(sem, "c_times_h_ready")
        m_summed = per_batch(sem, "c_times_h_summed")
        y0_ready = per_batch(sem, "y_lower_copied")
        ys_ready = per_batch(sem, "y_scan_copied")
        yback_done = per_batch(sem, "y_scan_transposed")
        fhid_done = per_batch(sem, "ffn_hidden_done")
        fhid_ready = per_batch(sem, "ffn_hidden_ready")
        h_ready = per_batch(sem, "h_ready")
        hb_ready = per_batch(sem, "h_plus_beta_ready")
        fused_done = sem("ffn_w2_wo_done")
        fused_ready = sem("ffn_w2_wo_copied")
        fout_done = per_batch(sem, "ffn_out_done")
        o_ready = per_batch(sem, "o_ready")

        block = ctx.enter_context(nc.Block())

        LNF, LN_SCAN, LN_FFN, LN_OUT = 2 * LAYERS, 2 * LAYERS + 1, 2 * LAYERS + 2, 2 * LAYERS + 3

        def col(c, n=1, r=P):
            return cols[0:r, c:c + n]

        def tiles_before(i):
            return NT * min(i, LN_SCAN) + 3 * max(0, i - LN_SCAN)

        def out_at(b, t):
            base = [0, W, BANK][t]
            return pa[b][0:ROWS[t], base:base + W]

        def parts(c):
            return P if c == 0 else W1

        NPAIR = NC_ // 2
        LEAD = 2
        PIPE = 2
        LAYER = ["k", "q", "v", "k_back", "q_norm", "ctx", "q_back", "ctx_outw", "att"]
        HALVES = ["k", "q", "v", "k_back", "q_norm", "q_back"]
        path = [("conv", g) for g in range(NG)]
        for l in range(LAYERS):
            path += [("stats", 2 * l), ("normed", 2 * l)]
            for s in LAYER:
                path += [(s, 2 * l), (s, 2 * l + 1)] if s in HALVES else [(s, 2 * l)]
            path += [("stats", 2 * l + 1), ("normed", 2 * l + 1)]
            path += [("ff1", 2 * l), ("ff1", 2 * l + 1), ("ff2", 2 * l), ("ff2", 2 * l + 1)]
        path += [("stats", LNF), ("normed", LNF), ("head", 0), ("h_stats", LN_SCAN), ("h_normed", LN_SCAN),
                 ("h_back", LN_SCAN), ("z", 0), ("bc", 0), ("softplus", 0), ("softplus", 1)]
        path += [("a_bar", c) for c in range(LEAD)]
        for p in range(NPAIR + PIPE):
            if p >= PIPE:
                path.append(("read", p - PIPE))
            if p < NPAIR:
                path.append(("expand", 2 * p))
            if p == 0:
                path.append(("spread_c", 0))
            elif PIPE <= p < NPAIR + 1:
                path.append(("spread_c", p - 1))
            if p < NPAIR:
                path.append(("expand", 2 * p + 1))
                path += [("a_bar", c) for c in (2 * p + LEAD, 2 * p + LEAD + 1) if c < NC_]
            if 1 <= p < NPAIR + 1:
                path += [("gain", 2 * p - 2), ("gain", 2 * p - 1), ("recur", p - 1)]
            if p > PIPE:
                path += [("sum", 2 * (p - PIPE) - 2), ("sum", 2 * (p - PIPE) - 1)]
            if 2 * p == C0 + 4:
                path.append(("y_lower", 0))
        path += [("sum", NC_ - 2), ("sum", NC_ - 1)]
        path += [("scan_out", 0), ("h_stats", LN_FFN), ("h_normed", LN_FFN), ("h_back", LN_FFN),
                 ("ffn_hidden", 0), ("ffn_out", 0), ("o_stats", LN_OUT), ("out", LN_OUT)]
        HAS = {
            "pe": ["text", "conv", "normed", "k", "q", "v", "k_back", "q_back", "ctx", "ctx_outw", "att", "ff1", "ff2",
                   "head", "h_normed", "expand", "spread_c", "sum", "scan_out", "ffn_out", "bc", "z", "ffn_hidden",
                   "fuse"],
            "dve": ["text_stats", "text_norm", "conv", "stats", "normed", "k", "q", "q_norm", "ctx", "ctx_outw", "att",
                    "ff2", "head", "h_stats", "h_normed", "bc", "z", "softplus", "gain", "recur", "read", "scan_out", "q_back",
                    "o_stats", "out", "fuse", "h_back"],
            "act": ["text", "normed", "k", "q", "v", "k_back", "q_back", "ctx", "ff1", "h_normed", "bc", "z", "softplus",
                    "a_bar", "expand", "y_lower", "scan_out", "ffn_hidden", "fuse"],
            "pool": ["h_back", "text_stats", "stats", "sums", "h_stats", "expand", "o_stats"],
        }

        AFTER = {("conv", NG - 1): ("text", 0, 0), ("k", 0): ("text_stats", 0, 0), ("att", 0): ("text_norm", 0, 0),
                 ("ff2", 2 * LAYERS - 1): ("fuse", 0, 0), ("stats", 1): ("sums", 0, 0), ("stats", 2): ("sums", 0, 1)}

        def order(engine):
            of = []
            for b in range(NB):
                mine = []
                for stage, i in path:
                    mine.append((stage, b, i))
                    if b == 0 and (stage, i) in AFTER:
                        mine.append(AFTER[stage, i])
                of.append([s for s in mine if s[0] in HAS[engine]])
            plan = [int(b) for b in PLAN[engine]]
            assert [plan.count(b) for b in range(NB)] == [len(s) for s in of]
            nxt = [iter(s) for s in of]
            return [next(nxt[b]) for b in plan]

        @block.sync
        def _(sp):
            sp.dma_start(ids_sb[:], ids).then_inc(s_ids, 16)
            for g, k in enumerate(GROUPS):
                sp.dma_start(convw_sb[:, k, :], convw[:, k, :]).then_inc(s_patch0[g], 16)
                sp.dma_start(patch_sb[0][:, k, :], patches[0, :, k, :]).then_inc(s_patch0[g], 16)
                if g == 1:
                    sp.dma_start(cols[:], cols_d).then_inc(s_cols, 16)
            sp.dma_start(ident[:], ident_d).then_inc(s_ident, 16)
            sp.dma_start(rows[:, 0:ROW_BO], rows_d[0:ROW_BO].partition_broadcast(P)).then_inc(s_rows, 16)
            for l in range(LAYERS):
                sp.dma_start(qkv_sb[:, l], qkvw[:, l]).then_inc(s_qkv[l], 16)
                if l == 0:
                    for g, k in enumerate(GROUPS):
                        sp.dma_start(patch_sb[1][:, k, :], patches[1, :, k, :]).then_inc(s_patch1[g], 16)
                sp.dma_start(outw_sb[:, l], outw[:, l]).then_inc(s_outw[l], 16)
                sp.dma_start(ff1_sb[:, l], ff1w[:, l]).then_inc(s_outw[l], 16)
                sp.dma_start(ff2_sb[:, l], ff2w[:, l]).then_inc(s_outw[l], 16)
            sp.dma_start(rows[:, ROW_BO:NROWS], rows_d[ROW_BO:NROWS].partition_broadcast(P)).then_inc(s_rows2, 16)
            sp.dma_start(misc[:], misc_d).then_inc(s_misc, 16)
            sp.dma_start(sel[:], sel_d).then_inc(s_sel, 16)
            for b in range(NB):
                sp.wait_ge(o_ready[b], NT)
                sp.dma_start(out[b, 0:TOK, :].rearrange("(t p) w -> p t w", p=P), o[b][:, 0:NT, :]).then_inc(s_out, 16)
                sp.wait_ge(o_ready[b], 3)
                sp.dma_start(out[b, TOK:L, :], o[b][0:S_TXT, NT, :]).then_inc(s_out, 16)
            sp.wait_ge(s_out, 2 * NB * 16)

        @block.gpsimd
        def _(pool):
            nc.gpsimd.memset(we[:, 0:1], 0.0)
            nc.gpsimd.memset(we[:, W + 1:W + 2], 0.0)
            nc.gpsimd.memset(pe_rows[:, 0:1], 0.0)
            nc.gpsimd.memset(pe_rows[:, W + 1:W + 2], 0.0).then_inc(s_edges, 1)
            pool.dma_start(tconst[:], tconst_d).then_inc(s_tconst, 16)
            for b in range(NB):
                pool.dma_start(pe_rows[b * S_TXT:(b + 1) * S_TXT, 1:W + 1], pos_emb[0:S_TXT, :]).then_inc(s_pos, 16)
            pool.wait_ge(s_ids, 16)
            pool.indirect_dma_start(out=we[:, 1:W + 1], out_offset=None, in_=word_emb,
                                    in_offset=bass.IndirectOffsetOnAxis(ap=ids_sb[:, 0:1], axis=0)).then_inc(s_word, 16)
            nc.gpsimd.memset(neghalf[:], -0.5).then_inc(s_fill, 1)
            pool.wait_ge(s_fill, 1)

            def inverse_root(b, i, tiles):
                pool.wait_ge(var_ready[b], i + 1)
                nc.gpsimd.tensor_tensor(rstd[b][:, 0:tiles], ve[b][:, 0:tiles], neghalf[:, 0:tiles],
                                        ALU.pow).then_inc(rstd_ready[b], 1)

            def add_bias(b, k, row):
                pool.wait_ge(x_ready[b], k)
                nc.gpsimd.tensor_tensor(xb[b][:], x[b][:],
                                        rows[:, row:row + D].unsqueeze(1).to_broadcast([P, NT, D]),
                                        ALU.add).then_inc(xb_ready[b], 1)

            pool.wait_ge(s_rows, 16)

            for stage, b, i in order("pool"):
                if stage == "text_stats":
                    pool.wait_ge(s_txtvar, 1)
                    nc.gpsimd.tensor_tensor(trstd[:], tve[:], neghalf[0:NB * S_TXT, 0:1], ALU.pow).then_inc(s_txtrstd, 1)
                elif stage == "stats":
                    inverse_root(b, i, NT)
                    if i < 2 * LAYERS:
                        add_bias(b, i + 1, (ROW_FF2B if i % 2 else ROW_OUTB) + (i // 2) * D)
                elif stage == "sums":
                    if i == 0:
                        pool.wait_ge(inv_ready, 1)
                        pool.wait_ge(s_ident, 16)
                        nc.gpsimd.tensor_tensor(sum0[:], ident[:].unsqueeze(1).to_broadcast([P, C0, P]),
                                                inv_a[:, 0:C0].unsqueeze(2).to_broadcast([P, C0, P]),
                                                ALU.mult).then_inc(sums_ready, 1)
                    else:
                        pool.wait_ge(s_misc, 16)
                        nc.gpsimd.tensor_tensor(sum1[:],
                                                misc[:, MI_FOLD:MI_FOLD + W1].unsqueeze(1).to_broadcast([P, C1, W1]),
                                                inv_a[:, C0:NC_].unsqueeze(2).to_broadcast([P, C1, W1]),
                                                ALU.mult).then_inc(sums_ready, 1)
                elif stage == "h_back" and i == LN_FFN:
                    pool.wait_ge(h_ready[b], 1)
                    pool.wait_ge(s_rows2, 16)
                    fb = rows[:, ROW_FB:ROW_FB + W]
                    nc.gpsimd.tensor_tensor(hb[b][:, 0:NT, :], h[b][:, 0:NT, :],
                                            fb.unsqueeze(1).to_broadcast([P, NT, W]), ALU.add)
                    nc.gpsimd.tensor_tensor(hb[b][0:S_TXT, NT, :], h[b][0:S_TXT, NT, :], fb[0:S_TXT, :],
                                            ALU.add).then_inc(hb_ready[b], 1)
                elif stage in ("h_stats", "o_stats"):
                    inverse_root(b, i, 3)
                elif stage == "expand":
                    pool.wait_ge(b_copied[b], i + 1)
                    if i >= RU:
                        pool.wait_ge(binc_ready[b], i - RU + 1)
                    nc.gpsimd.tensor_tensor(u[b][:, i % RU, :], bsp[b][:, i % RS, :],
                                            ht[b][:, 0 if i < C0 else 1, :], ALU.mult).then_inc(u_ready[b], 1)

        @block.vector
        def _(dve):
            steps = [0]

            def mark(ins):
                steps[0] += 1
                ins.then_inc(dve_step, 1)
                return steps[0]

            def link(ins):
                dve.wait_ge(dve_step, mark(ins))

            def norm_stats(b, i, src, width, tiles, eps):
                variances(b, [mark(nc.vector.bn_stats(stats[b][0:ROWS[t], t, :], src[0:ROWS[t], t, 0:width]))
                              for t in range(tiles)], eps)

            def variances(b, taken, eps=EPS):
                tiles = len(taken)
                for t in range(tiles):
                    dve.wait_ge(dve_step, taken[t])
                    last = nc.vector.bn_aggr(mv[b][0:ROWS[t], t, :], stats[b][0:ROWS[t], t, :])
                link(last)
                nc.vector.tensor_scalar(ve[b][:, 0:tiles], mv[b][:, 0:tiles, 1], eps, None,
                                        ALU.add).then_inc(var_ready[b], 1)

            def normalise(b, i, dst, src, width, tiles, each=True):
                dve.wait_ge(rstd_ready[b], i + 1)
                for t in range(tiles):
                    r = ROWS[t]
                    last = nc.vector.tensor_scalar(dst[0:r, t, 0:width], src[0:r, t, 0:width], mv[b][0:r, t, 0:1],
                                                   rstd[b][0:r, t:t + 1], ALU.subtract, ALU.mult)
                    if each:
                        last.then_inc(xn_ready[b], 1)
                return last

            for b in range(NB):
                nc.vector.memset(ctxt[b][:], 0.0)
                last = nc.vector.memset(mv[b][:], 1.0)
            link(last)
            dve.wait_ge(s_cols, 16)
            dve.wait_ge(s_tconst, 16)
            for i in range(3):
                shift = tconst[:, i * 2 * S_TXT:(i + 1) * 2 * S_TXT].unsqueeze(1).to_broadcast([2 * S_TXT, 6, 2 * S_TXT])
                taps = col(COL_CW + 6 * i, 6, 2 * S_TXT).unsqueeze(2).to_broadcast([2 * S_TXT, 6, 2 * S_TXT])
                link(nc.vector.tensor_tensor((band if i == 0 else band_t)[:], shift, taps, ALU.mult))
                if i:
                    ins = nc.vector.tensor_tensor(band[:], band[:], band_t[:], ALU.add)
                    if i == 1:
                        link(ins)
                    else:
                        ins.then_inc(s_band, 1)
            nc.vector.reciprocal(inv_a[:], col(COL_A, NC_)).then_inc(inv_ready, 1)
            nc.vector.tensor_tensor(pdelta[:], col(COL_PD, 2), col(COL_BD).to_broadcast([P, 2]),
                                    ALU.add).then_inc(pdelta_ready, 1)
            for stage, b, i in order("dve"):
                l, half = i // 2, i % 2
                tile = slice(half * NH, (half + 1) * NH)
                if stage == "text_stats":
                    dve.wait_ge(s_txtgelu, 1)
                    link(nc.vector.bn_stats(tstats[:], txt[:]))
                    link(nc.vector.bn_aggr(tmv[:], tstats[:]))
                    nc.vector.tensor_scalar(tve[:], tmv[:, 1:2], EPS_TXT, None, ALU.add).then_inc(s_txtvar, 1)
                elif stage == "text_norm":
                    dve.wait_ge(s_txtrstd, 1)
                    dve.wait_ge(s_rows2, 16)
                    link(nc.vector.tensor_scalar(txt[:], txt[:], tmv[:, 0:1], trstd[:], ALU.subtract, ALU.mult))
                    link(nc.vector.tensor_tensor(txt[:], txt[:], rows[0:NB * S_TXT, ROW_TG:ROW_TG + W], ALU.mult))
                    for tb in range(NB):
                        r = slice(tb * S_TXT, (tb + 1) * S_TXT)
                        last = nc.vector.tensor_tensor(h[tb][0:S_TXT, NT, :], txt[r, :], rows[r, ROW_TB:ROW_TB + W],
                                                       ALU.add)
                    link(last)
                elif stage == "conv" and i == NG - 1:
                    dve.wait_ge(conv_done[b], 1)
                    dve.wait_ge(s_rows, 16)
                    nc.vector.tensor_tensor(x[b][:], pa[b][:].rearrange("p (t w) -> p t w", t=NT)[:, :, 0:D],
                                            rows[:, ROW_CONVB:ROW_CONVB + D].unsqueeze(1).to_broadcast([P, NT, D]),
                                            ALU.add).then_inc(x_ready[b], 1)
                elif stage == "stats":
                    dve.wait_ge(x_ready[b], i + 1)
                    norm_stats(b, i, x[b], D, NT, EPS)
                elif stage == "normed":
                    normalise(b, i, xn[b], x[b], D, NT)
                elif stage == "k":
                    j = slice(2 * half, 2 * half + 2)
                    dve.wait_ge(kt_done[b], i + 1)
                    nc.vector.tensor_reduce(kmax[b][:, j], pb[b][:].rearrange("p (j n) -> p j n", j=NJ)[:, j, :], AX,
                                            ALU.max, negate=True).then_inc(kmax_ready[b], 1)
                elif stage == "q":
                    dve.wait_ge(q_done[b], i + 1)
                    src = pa[b][:].rearrange("p (h d) -> p h d", d=DH)[:, tile, :]
                    link(nc.vector.tensor_reduce(qmax[b][:, tile], src, AX, ALU.max))
                    nc.vector.tensor_tensor(q[b][:, tile, :], src, qmax[b][:, tile].unsqueeze(2).to_broadcast([P, NH, DH]),
                                            ALU.subtract).then_inc(qsub_ready[b], 1)
                elif stage == "q_norm":
                    dve.wait_ge(eq_ready[b], i + 1)
                    summed = mark(nc.vector.tensor_reduce(qmax[b][:, tile], q[b][:, tile, :], AX, ALU.add))
                    if half == 1:
                        dve.wait_ge(ek_ready[b], 2 * l + 2)
                        k_rec = mark(nc.vector.reciprocal(krec[b][:], ksum[b][:]))
                        dve.wait_ge(dve_step, summed)
                        q_rec = mark(nc.vector.reciprocal(qrec[b][:], qmax[b][:]))
                        dve.wait_ge(dve_step, k_rec)
                        nc.vector.tensor_scalar(krec[b][:], krec[b][:], DH ** -0.5, None, ALU.mult)
                        dve.wait_ge(dve_step, q_rec)
                        for t in range(NT):
                            heads = slice(t * NH, (t + 1) * NH)
                            nc.vector.tensor_tensor(q[b][:, heads, :], q[b][:, heads, :],
                                                    qrec[b][:, heads].unsqueeze(2).to_broadcast([P, NH, DH]),
                                                    ALU.mult).then_inc(qn_ready[b], 1)
                elif stage == "q_back" and half == 1:
                    dve.wait_ge(qt_done[b], i + 1)
                    nc.vector.tensor_copy(qt[b][:].rearrange("p j n -> p (j n)")[:, BANK:2 * BANK],
                                          pb[b][:, BANK:2 * BANK]).then_inc(qt_ready[b], 1)
                elif stage == "ctx":
                    dve.wait_ge(ctx_done[b], l + 1)
                    r = slice(DH, 2 * DH)
                    nc.vector.tensor_copy(ctxt[b][r, :, r], pa[b][r, 0:BANK].rearrange("p (j d) -> p j d", j=NJ)[:, :, r]
                                          ).then_inc(ctx1_ready[b], 1)
                elif stage == "ctx_outw":
                    dve.wait_ge(cw_done[b], l + 1)
                    nc.vector.tensor_tensor(cw[b][:], pa[b][:, BANK:2 * BANK].rearrange("p (j d) -> p j d", j=NJ),
                                            krec[b][:].unsqueeze(2).to_broadcast([P, NJ, D]),
                                            ALU.mult).then_inc(cw_ready[b], 1)
                elif stage == "att":
                    dve.wait_ge(att_done[b], l + 1)
                    dve.wait_ge(xb_ready[b], 2 * l + 1)
                    nc.vector.tensor_tensor(x[b][:], pb[b][:, 0:NT * D].rearrange("p (t d) -> p t d", t=NT), xb[b][:],
                                            ALU.add).then_inc(x_ready[b], 1)
                elif stage == "ff2" and half == 1:
                    dve.wait_ge(ff2_done[b], l + 1)
                    dve.wait_ge(xb_ready[b], 2 * l + 2)
                    nc.vector.tensor_tensor(x[b][:], pa[b][:].rearrange("p (t w) -> p t w", t=NT)[:, :, 0:D], xb[b][:],
                                            ALU.add).then_inc(x_ready[b], 1)
                elif stage == "head":
                    for slots in (abar[b], binc[b]):
                        nc.vector.memset(slots[:, 1::2, 0:1], 0.0)
                    dve.wait_ge(head_done[b], 1)
                    link(nc.vector.tensor_tensor(h[b][:, 0:NT, :],
                                                 pb[b][:].rearrange("p (t w) -> p t w", t=NT)[:, :, 0:W],
                                                 rows[:, ROW_HEADB:ROW_HEADB + W].unsqueeze(1).to_broadcast([P, NT, W]),
                                                 ALU.add))
                elif stage == "h_stats":
                    if i == LN_FFN:
                        dve.wait_ge(h_ready[b], 1)
                    norm_stats(b, i, h[b], W, 3, EPS)
                elif stage == "h_normed":
                    normalise(b, i, hn[b], h[b], W if i == LN_FFN else P, 3, each=i == LN_FFN)
                    if i == LN_SCAN:
                        for t in range(3):
                            r = ROWS[t]
                            nc.vector.tensor_scalar(
                                hn[b][0:r, t, P:2 * P].rearrange("p (c w) -> p c w", c=2),
                                h[b][0:r, t, P:W].unsqueeze(1).to_broadcast([r, 2, W1]), mv[b][0:r, t, 0:1],
                                rstd[b][0:r, t:t + 1], ALU.subtract, ALU.mult).then_inc(xn_ready[b], 1)
                elif stage == "h_back":
                    r = P if i == LN_SCAN else W1
                    dve.wait_ge(tr_done[b], i + 1)
                    nc.vector.tensor_copy(ht[b][0:r, 1, :], pa[b][0:r, BANK:BANK + L]).then_inc(yt_ready[b], 1)
                elif stage == "bc":
                    K = 2 * N
                    dve.wait_ge(bc_ready[b], 2)
                    nc.vector.tensor_tensor(bcr[b][K:2 * K, :], bc[b][:], bc3[b][0:K, :], ALU.subtract)
                    link(nc.vector.tensor_tensor(bc3[b][K:2 * K, :], bc[b][:], bc3[b][0:K, :], ALU.subtract))
                    nc.vector.tensor_tensor(bc3[b][2 * K:3 * K, :], bcr[b][K:2 * K, :], bc3[b][K:2 * K, :],
                                            ALU.subtract).then_inc(bc3_ready[b], 1)
                elif stage == "z":
                    dve.wait_ge(zabs_ready[b], 1)
                    for c in range(2):
                        last = nc.vector.tensor_scalar(z[b][:, c, :], pb[b][:, BANK:BANK + L], pdelta[:, c:c + 1], 0.0,
                                                       ALU.add, ALU.max)
                    last.then_inc(z_read[b], 1)
                elif stage == "softplus":
                    dve.wait_ge(z_read[b], 1)
                    dve.wait_ge(lnz_ready[b], i + 1)
                    nc.vector.tensor_tensor(delta[b][:, i, :], z[b][:, i, :], ez[b][:, i, :],
                                            ALU.add).then_inc(delta_ready[b], 1)
                elif stage == "gain":
                    dve.wait_ge(u_ready[b], i + 1)
                    dve.wait_ge(abar_ready[b], i + 1)
                    if i >= RB:
                        dve.wait_ge(hs_ready[b], i // 2 * 2 - RB + 2)
                    nc.vector.scalar_tensor_tensor(binc[b][:, i % RB, 1:], abar[b][:, i % RA, 1:], col(COL_A + i),
                                                   u[b][:, i % RU, :], ALU.subtract,
                                                   ALU.mult).then_inc(binc_ready[b], 1)
                elif stage == "recur":
                    c = 2 * i
                    dve.wait_ge(binc_ready[b], c + 2)
                    if c >= RH:
                        dve.wait_ge(m_ready[b], c - RH + 2)
                    nc.vector.tensor_tensor_scan(through(hs[b], c % RH), through(abar[b], c % RA), through(binc[b], c % RB),
                                                 0.0, ALU.mult, ALU.add).then_inc(hs_ready[b], 2)
                elif stage == "read":
                    c = 2 * i
                    dve.wait_ge(hs_ready[b], c + 2)
                    dve.wait_ge(c_spread[b], c + 2)
                    if c >= RM:
                        dve.wait_ge(m_summed[b], c - RM + 2)
                    nc.vector.tensor_tensor(m[b][:, c % RM:c % RM + 2, :], hs[b][:, c % RH:c % RH + 2, 1:],
                                            pb[b][:].rearrange("p (c n) -> p c n", c=2)[:, :, 0:L],
                                            ALU.mult).then_inc(m_ready[b], 2)
                elif stage == "scan_out":
                    dve.wait_ge(yback_done[b], 1)
                    nc.vector.tensor_tensor(h[b][:, 0:NT, :], h[b][:, 0:NT, :],
                                            pb[b][:, 0:NT * W].rearrange("p (t w) -> p t w", t=NT), ALU.add)
                    nc.vector.tensor_tensor(h[b][0:S_TXT, NT, :], h[b][0:S_TXT, NT, :],
                                            pb[b][0:S_TXT, BANK:BANK + W], ALU.add).then_inc(h_ready[b], 1)
                elif stage == "fuse":
                    dve.wait_ge(s_rows2, 16)
                    dve.wait_ge(fused_done, 1)
                    nc.vector.tensor_tensor(bo2[:], pb[0][:, 0:W], rows[:, ROW_BO:ROW_BO + W],
                                            ALU.add).then_inc(fused_ready, 1)
                elif stage == "o_stats":
                    dve.wait_ge(fout_done[b], 3)
                    variances(b, [mark(nc.vector.bn_stats(stats[b][0:ROWS[t], t, :], out_at(b, t)))
                                  for t in range(3)])
                    fg = rows[:, ROW_FG:ROW_FG + W]
                    for t in range(3):
                        r = ROWS[t]
                        last = nc.vector.scalar_tensor_tensor(o[b][0:r, t, :], out_at(b, t), mv[b][0:r, t, 0:1],
                                                              fg[0:r, :], ALU.subtract, ALU.mult)
                    link(last)
                elif stage == "out":
                    dve.wait_ge(hb_ready[b], 1)
                    dve.wait_ge(rstd_ready[b], i + 1)
                    for t in range(3):
                        r = ROWS[t]
                        nc.vector.scalar_tensor_tensor(o[b][0:r, t, :], o[b][0:r, t, :], rstd[b][0:r, t:t + 1],
                                                       hb[b][0:r, t, :], ALU.mult, ALU.add).then_inc(o_ready[b], 1)

        @block.scalar
        def _(act):
            steps = [0]

            def link(ins):
                steps[0] += 1
                ins.then_inc(act_step, 1)
                act.wait_ge(act_step, steps[0])

            def affine(b, i, c):
                act.wait_ge(tr_done[b], i + 1)
                nc.scalar.activation(yt[b][:], pa[b][:, 0:TOK], ACT.Identity, bias=col(c + 1),
                                     scale=col(c)).then_inc(yt_ready[b], 1)

            loaded = [None]

            def tables(name):
                if loaded[0] != name:
                    nc.scalar.preload_act_table_set(name)
                    loaded[0] = name

            tables("gelu_and_others")
            act.wait_ge(s_cols, 16)

            for stage, b, i in order("act"):
                l, half = i // 2, i % 2
                if stage == "text":
                    act.wait_ge(s_txtconv, 1)
                    nc.scalar.activation(txt[:], pb[0][0:NB * S_TXT, 0:W], ACT.Gelu).then_inc(s_txtgelu, 1)
                    tables("natural_log_exp_and_others")
                elif stage == "normed":
                    affine(b, i, COL_LNF if i == 2 * LAYERS else COL_LN + 2 * i)
                elif stage == "k":
                    tables("natural_log_exp_and_others")
                    act.wait_ge(kmax_ready[b], i + 1)
                    for j in range(2 * half, 2 * half + 2):
                        last = nc.scalar.activation(ekt[b][:, j, :], pb[b][:, j * TOK:(j + 1) * TOK], ACT.Exp,
                                                    bias=kmax[b][:, j:j + 1], accum_out=ksum[b][:, j:j + 1])
                    last.then_inc(ek_ready[b], 1)
                elif stage == "q":
                    tables("natural_log_exp_and_others")
                    act.wait_ge(qsub_ready[b], i + 1)
                    tile = slice(half * NH, (half + 1) * NH)
                    nc.scalar.activation(q[b][:, tile, :], q[b][:, tile, :], ACT.Exp).then_inc(eq_ready[b], 1)
                elif stage == "v":
                    act.wait_ge(v_done[b], i + 1)
                    nc.scalar.activation(v[b][:, half, :], pb[b][:, half * BANK:(half + 1) * BANK],
                                         ACT.Copy).then_inc(v_ready[b], 1)
                elif stage == "k_back":
                    act.wait_ge(kn_done[b], i + 1)
                    nc.scalar.activation(kn[b][:, half, :], pa[b][:, half * BANK:(half + 1) * BANK],
                                         ACT.Copy).then_inc(kn_ready[b], 1)
                elif stage == "q_back" and half == 0:
                    act.wait_ge(qt_done[b], i + 1)
                    nc.scalar.activation(qt[b][:].rearrange("p j n -> p (j n)")[:, 0:BANK], pb[b][:, 0:BANK],
                                         ACT.Copy).then_inc(qt0_ready[b], 1)
                elif stage == "ctx":
                    act.wait_ge(ctx_done[b], l + 1)
                    nc.scalar.activation(ctxt[b][0:DH, :, 0:DH],
                                         pa[b][0:DH, 0:BANK].rearrange("p (j d) -> p j d", j=NJ)[:, :, 0:DH],
                                         ACT.Copy).then_inc(ctx0_ready[b], 1)
                elif stage == "ff1":
                    tables("gelu_and_others")
                    act.wait_ge(ff1_done[b], i + 1)
                    for k in range(2 * half, 2 * half + 2):
                        last = nc.scalar.activation(hid[b][:, k, :], pb[b][:, k * TOK:(k + 1) * TOK], ACT.Gelu,
                                                    bias=col(COL_FF1B + NM * l + k))
                    last.then_inc(gelu_done[b], 1)
                elif stage == "h_normed":
                    act.wait_ge(tr_done[b], i + 1)
                    nc.scalar.activation(ht[b][:, 0, :], pa[b][:, 0:L], ACT.Copy).then_inc(yt_ready[b], 1)
                elif stage == "bc":
                    act.wait_ge(bc_done[b], 1)
                    nc.scalar.activation(bc[b][:], pb[b][0:2 * N, 0:L], ACT.Identity,
                                         bias=col(COL_BBC, 1, 2 * N)).then_inc(bc_ready[b], 1)
                    nc.scalar.activation(bc3[b][0:2 * N, :], pb[b][0:2 * N, 0:L], ACT.Identity,
                                         bias=col(COL_BBC, 1, 2 * N)).then_inc(bc_ready[b], 1)
                elif stage == "z":
                    act.wait_ge(z_done[b], 1)
                    act.wait_ge(pdelta_ready, 1)
                    for c in range(2):
                        last = nc.scalar.activation(ez[b][:, c, :], pb[b][:, BANK:BANK + L], ACT.Abs,
                                                    bias=pdelta[:, c:c + 1])
                    last.then_inc(zabs_ready[b], 1)
                elif stage == "softplus":
                    tables("natural_log_exp_and_others")
                    act.wait_ge(zabs_ready[b], 1)
                    link(nc.scalar.activation(ez[b][:, i, :], ez[b][:, i, :], ACT.Exp, scale=-1.0))
                    nc.scalar.activation(ez[b][:, i, :], ez[b][:, i, :], ACT.Ln, bias=1.0).then_inc(lnz_ready[b], 1)
                elif stage == "a_bar":
                    if i in (0, C0):
                        act.wait_ge(delta_ready[b], 1 if i == 0 else 2)
                    tables("natural_log_exp_and_others")
                    if i >= RA:
                        act.wait_ge(hs_ready[b], (i - RA) // 2 * 2 + 2)
                    nc.scalar.activation(abar[b][:, i % RA, 1:], delta[b][:, 0 if i < C0 else 1, :], ACT.Exp,
                                         scale=col(COL_A + i)).then_inc(abar_ready[b], 1)
                elif stage == "expand":
                    act.wait_ge(b_spread[b], i + 1)
                    if i >= RS:
                        act.wait_ge(u_ready[b], i - RS + 1)
                    nc.scalar.activation(bsp[b][:, i % RS, :], pa[b][:, BANK:BANK + L],
                                         ACT.Copy).then_inc(b_copied[b], 1)
                elif stage == "y_lower":
                    act.wait_ge(m_summed[b], C0)
                    nc.scalar.activation(ys[b][:, 0, :], pa[b][:, 0:L], ACT.Copy).then_inc(y0_ready[b], 1)
                elif stage == "scan_out":
                    act.wait_ge(m_summed[b], NC_)
                    nc.scalar.activation(ys[b][0:W1, 1, :], pa[b][0:W1, 0:L],
                                         ACT.Copy).then_inc(ys_ready[b], 1)
                elif stage == "ffn_hidden":
                    act.wait_ge(fhid_done[b], 1)
                    nc.scalar.activation(fhid[b][:], pb[b][:, 0:L], ACT.Relu,
                                         bias=col(COL_B1)).then_inc(fhid_ready[b], 1)
                elif stage == "fuse":
                    act.wait_ge(fused_done, 1)
                    nc.scalar.activation(w2o[:], pb[0][:, BANK:BANK + W], ACT.Copy).then_inc(fused_ready, 1)

        @block.tensor
        def _(pe):
            def mm(dst, lhs_t, rhs, first=True, last=True):
                return nc.tensor.matmul(dst, lhs_t, rhs, start=first, stop=last)

            def to_features(b, i):
                for t in range(NT):
                    pe.wait_ge(xn_ready[b], tiles_before(i) + t + 1)
                    last = nc.tensor.transpose(pa[b][:, t * P:(t + 1) * P], xn[b][:, t, :], ident[:])
                last.then_inc(tr_done[b], 1)

            def h_to_features(b, i, second):
                for t in range(3):
                    pe.wait_ge(xn_ready[b], tiles_before(i) + t + 1)
                    r = ROWS[t]
                    nc.tensor.transpose(pa[b][:, t * P:t * P + r], hn[b][0:r, t, 0:P], ident[0:r, 0:r])
                    last = nc.tensor.transpose(pa[b][0:second, BANK + t * P:BANK + t * P + r],
                                               hn[b][0:r, t, P:P + second], ident[0:r, 0:r])
                last.then_inc(tr_done[b], 1)

            def spread_b(b, c):
                if c:
                    pe.wait_ge(b_copied[b], c)
                mm(pa[b][:, BANK:BANK + L], sel[:, 2 * c, :], bc3[b][:]).then_inc(b_spread[b], 1)

            def spread_c(b, p):
                if p:
                    pe.wait_ge(m_ready[b], 2 * p)
                for e in range(2):
                    last = mm(pb[b][:, e * BANK:e * BANK + L], sel[:, 2 * (2 * p + e) + 1, :], bc3[b][:])
                last.then_inc(c_spread[b], 2)

            def sum_m(b, c):
                pe.wait_ge(m_ready[b], c + 1)
                src = m[b][:, c % RM, :]
                if c < C0:
                    mm(pa[b][:, 0:L], sum0[:, c, :], src, c == 0, c == C0 - 1).then_inc(m_summed[b], 1)
                else:
                    if c == C0:
                        pe.wait_ge(y0_ready[b], 1)
                    mm(pa[b][0:W1, 0:L], sum1[:, c - C0, :], src, c == C0, c == NC_ - 1).then_inc(m_summed[b], 1)

            for stage, b, i in order("pe"):
                l, half = i // 2, i % 2
                tile = slice(half * P, (half + 1) * P)
                if stage == "text":
                    pe.wait_ge(s_band, 1)
                    pe.wait_ge(s_edges, 1)
                    pe.wait_ge(s_pos, 16 * NB)
                    pe.wait_ge(s_word, 16)
                    for k in range(6):
                        src = we if k < 3 else pe_rows
                        last = mm(pb[0][0:NB * S_TXT, 0:W], band[:, k, :], src[:, k % 3:k % 3 + W], k == 0, k == 5)
                    last.then_inc(s_txtconv, 1)
                elif stage == "conv":
                    if b == 0:
                        pe.wait_ge(s_patch0[i], 2 * 16)
                    else:
                        pe.wait_ge(s_patch1[i], 16)
                    for k in range(KT)[GROUPS[i]]:
                        for t in range(NT):
                            last = mm(pa[b][:, t * BANK:t * BANK + D], patch_sb[b][:, k, t * P:(t + 1) * P],
                                      convw_sb[:, k, :], k == 0, k == KT - 1)
                    if i == NG - 1:
                        last.then_inc(conv_done[b], 1)
                elif stage == "normed":
                    if i == 0:
                        pe.wait_ge(s_ident, 16)
                    to_features(b, i)
                elif stage == "k":
                    if half == 0:
                        pe.wait_ge(yt_ready[b], 2 * l + 1)
                        pe.wait_ge(s_qkv[l], 16)
                        if l == 0:
                            pe.wait_ge(s_txtgelu, 1)
                    for j in range(2 * half, 2 * half + 2):
                        last = mm(pb[b][:, j * TOK:(j + 1) * TOK], qkv_sb[:, l, INNER + j * P:INNER + (j + 1) * P],
                                  yt[b][:])
                    last.then_inc(kt_done[b], 1)
                elif stage == "q":
                    mm(pa[b][:, half * BANK:(half + 1) * BANK], yt[b][:, tile],
                       qkv_sb[:, l, 0:INNER]).then_inc(q_done[b], 1)
                elif stage == "v":
                    pe.wait_ge(ek_ready[b], i + 1)
                    mm(pb[b][:, half * BANK:(half + 1) * BANK], yt[b][:, tile],
                       qkv_sb[:, l, 2 * INNER:3 * INNER]).then_inc(v_done[b], 1)
                elif stage == "k_back":
                    pe.wait_ge(qsub_ready[b], i + 1)
                    pe.wait_ge(ek_ready[b], 2 * l + 2)
                    for j in range(NJ):
                        last = nc.tensor.transpose(pa[b][:, half * BANK + j * P:half * BANK + (j + 1) * P],
                                                   ekt[b][:, j, tile], ident[:])
                    last.then_inc(kn_done[b], 1)
                elif stage == "q_back":
                    pe.wait_ge(qn_ready[b], 2 * l + 2)
                    pe.wait_ge(v_ready[b], i + 1)
                    qv = q[b][:].rearrange("p (t e) d -> p t (e d)", t=NT)
                    for j in range(2 * half, 2 * half + 2):
                        for t in range(NT):
                            last = nc.tensor.transpose(pb[b][:, j * TOK + t * P:j * TOK + (t + 1) * P],
                                                       qv[:, t, j * P:(j + 1) * P], ident[:])
                    last.then_inc(qt_done[b], 1)
                elif stage == "ctx":
                    pe.wait_ge(kn_ready[b], 2 * l + 2)
                    pe.wait_ge(v_ready[b], 2 * l + 2)
                    for j in range(NJ):
                        for t in range(NT):
                            last = mm(pa[b][:, j * P:(j + 1) * P], v[b][:, t, j * P:(j + 1) * P],
                                      kn[b][:, t, j * P:(j + 1) * P], t == 0, t == NT - 1)
                    last.then_inc(ctx_done[b], 1)
                elif stage == "ctx_outw":
                    pe.wait_ge(ctx0_ready[b], l + 1)
                    pe.wait_ge(ctx1_ready[b], l + 1)
                    pe.wait_ge(s_outw[l], 3 * 16)
                    for j in range(NJ):
                        last = mm(pa[b][:, BANK + j * D:BANK + (j + 1) * D], ctxt[b][:, j, :], outw_sb[:, l, j, :])
                    last.then_inc(cw_done[b], 1)
                elif stage == "att":
                    pe.wait_ge(cw_ready[b], l + 1)
                    pe.wait_ge(qt0_ready[b], l + 1)
                    pe.wait_ge(qt_ready[b], l + 1)
                    for t in range(NT):
                        for j in range(NJ):
                            last = mm(pb[b][:, t * D:(t + 1) * D], qt[b][:, j, t * P:(t + 1) * P], cw[b][:, j, :],
                                      j == 0, j == NJ - 1)
                    last.then_inc(att_done[b], 1)
                elif stage == "ff1":
                    if half == 0:
                        pe.wait_ge(yt_ready[b], 2 * l + 2)
                    for k in range(2 * half, 2 * half + 2):
                        last = mm(pb[b][:, k * TOK:(k + 1) * TOK], ff1_sb[:, l, k * P:(k + 1) * P], yt[b][:])
                    last.then_inc(ff1_done[b], 1)
                elif stage == "ff2":
                    pe.wait_ge(gelu_done[b], i + 1)
                    for k in range(2 * half, 2 * half + 2):
                        for t in range(NT):
                            last = mm(pa[b][:, t * BANK:t * BANK + D], hid[b][:, k, t * P:(t + 1) * P],
                                      ff2_sb[:, l, k, :], k == 0, k == NM - 1)
                    if half == 1:
                        last.then_inc(ff2_done[b], 1)
                elif stage == "head":
                    pe.wait_ge(yt_ready[b], LNF + 1)
                    if b == 0:
                        pe.wait_ge(fused_ready, 2)
                    pe.wait_ge(s_misc, 16)
                    for t in range(NT):
                        last = mm(pb[b][:, t * BANK:t * BANK + W], yt[b][:, t * P:(t + 1) * P],
                                  misc[:, MI_HEAD:MI_HEAD + W])
                    last.then_inc(head_done[b], 1)
                elif stage == "h_normed":
                    h_to_features(b, i, P if i == LN_SCAN else W1)
                elif stage == "z":
                    pe.wait_ge(yt_ready[b], LNF + 1 + 2)
                    for c in range(2):
                        r = parts(c)
                        last = mm(pb[b][:, BANK:BANK + L], misc[0:r, MI_WD + P * c:MI_WD + P * (c + 1)],
                                  ht[b][0:r, c, :], c == 0, c == 1)
                    last.then_inc(z_done[b], 1)
                elif stage == "bc":
                    for c in range(2):
                        r = parts(c)
                        last = mm(pb[b][0:2 * N, 0:L], misc[0:r, MI_BC + 2 * N * c:MI_BC + 2 * N * (c + 1)],
                                  ht[b][0:r, c, :], c == 0, c == 1)
                    last.then_inc(bc_done[b], 1)
                elif stage == "expand":
                    if i == 0:
                        pe.wait_ge(bc3_ready[b], 1)
                        pe.wait_ge(s_sel, 16)
                    spread_b(b, i)
                elif stage == "spread_c":
                    if i == 0:
                        pe.wait_ge(z_read[b], 1)
                    spread_c(b, i)
                elif stage == "sum":
                    if i == 0:
                        pe.wait_ge(sums_ready, 2)
                    sum_m(b, i)
                elif stage == "scan_out":
                    pe.wait_ge(m_ready[b], NC_)
                    pe.wait_ge(y0_ready[b], 1)
                    for t in range(3):
                        r = ROWS[t]
                        base = t * W if t < NT else BANK
                        nc.tensor.transpose(pb[b][0:r, base:base + P], ys[b][:, 0, t * P:t * P + r], ident[:])
                    pe.wait_ge(ys_ready[b], 1)
                    for t in range(3):
                        r = ROWS[t]
                        base = t * W if t < NT else BANK
                        last = nc.tensor.transpose(pb[b][0:r, base + P:base + W], ys[b][0:W1, 1, t * P:t * P + r],
                                                   ident[0:W1, 0:W1])
                    last.then_inc(yback_done[b], 1)
                elif stage == "ffn_hidden":
                    pe.wait_ge(yt_ready[b], LNF + 1 + 4)
                    for c in range(2):
                        r = parts(c)
                        last = mm(pb[b][:, 0:L], misc[0:r, MI_W1 + FFI * c:MI_W1 + FFI * (c + 1)], ht[b][0:r, c, :],
                                  c == 0, c == 1)
                    last.then_inc(fhid_done[b], 1)
                elif stage == "fuse":
                    pe.wait_ge(s_misc, 16)
                    pe.wait_ge(gelu_done[0], 2 * LAYERS)
                    for c in range(2):
                        k = parts(c)
                        mm(pb[0][:, 0:W], col(COL_B2 + c, 1, k).to_broadcast([k, P]),
                           misc[0:k, MI_WO + W * c:MI_WO + W * (c + 1)], c == 0, c == 1)
                    for c in range(2):
                        k = parts(c)
                        last = mm(pb[0][:, BANK:BANK + W], misc[0:k, MI_W2 + FFI * c:MI_W2 + FFI * (c + 1)],
                                  misc[0:k, MI_WO + W * c:MI_WO + W * (c + 1)], c == 0, c == 1)
                    last.then_inc(fused_done, 1)
                elif stage == "ffn_out":
                    pe.wait_ge(fused_ready, 2)
                    pe.wait_ge(fhid_ready[b], 1)
                    for t in range(3):
                        r = ROWS[t]
                        mm(out_at(b, t), ident[:, 0:r], bo2[:], True, False)
                        mm(out_at(b, t), fhid[b][:, t * P:t * P + r], w2o[:], False, True).then_inc(fout_done[b], 1)


def kernel(**inputs):
    import concourse.bacc as bacc
    import ml_dtypes
    from concourse.bass_utils import run_bass_kernel_spmd

    a = {k: np.asarray(x) for k, x in inputs.items()}
    f32 = np.float32

    def two_parts(w):
        second = np.zeros((P, w.shape[1]), f32)
        second[:W1] = w[P:]
        return np.concatenate([w[:P], second], axis=1)

    def column(v, rows=P):
        c = np.zeros((P, 1), f32)
        c[:rows, 0] = v
        return c

    x = a["x"].reshape(NB, 32, 16, 8, 16, 8)
    patches = x.transpose(0, 1, 3, 5, 2, 4).reshape(NB, KT, P, TOK).transpose(0, 2, 1, 3)
    convw = a["L0_tok_conv_w"].reshape(D, KT, P).transpose(2, 1, 0)
    qkvw = a["L0_tok_qkv_w"].transpose(1, 0, 2)
    outw = a["L0_tok_out_w"].reshape(LAYERS, NJ, P, D).transpose(2, 0, 1, 3)
    ff1w = a["L0_tok_ff1_w"].transpose(1, 0, 2)
    ff2w = a["L0_tok_ff2_w"].reshape(LAYERS, NM, P, D).transpose(2, 0, 1, 3)

    cols = []
    for l in range(LAYERS):
        for n in ("ln1_g", "ln1_b", "ln2_g", "ln2_b"):
            cols.append(column(a["L0_tok_" + n][l]))
    cols += [column(a["L0_tok_lnf_g"]), column(a["L0_tok_lnf_b"])]
    cols.append(a["L0_tok_ff1_b"].reshape(LAYERS * NM, P).T)
    cols.append(column(np.concatenate([a["L0_attn_b_B"], a["L0_attn_b_C"]]), 2 * N))
    cols.append(column(a["L0_ffn_b1"]))
    cols += [column(a["L0_ffn_b2"][:P]), column(a["L0_ffn_b2"][P:], W1)]
    pd = a["L0_attn_p_Delta"]
    cols += [column(pd[:P]), column(np.tile(pd[P:], 2))]
    cols.append(np.broadcast_to(a["L0_attn_b_D"].reshape(1, 1), (P, 1)))
    aa = a["L0_attn_A"]
    cols.append(aa[:P])
    cols.append(np.concatenate([aa[P:, :C1], aa[P:, C1:]], axis=0))
    taps = a["L0_txt_conv_w"][0].transpose(1, 0, 2).reshape(1, 18)
    cols.append(np.broadcast_to(taps, (P, 18)))
    cols = np.ascontiguousarray(np.concatenate(cols, axis=1))
    assert cols.shape == (P, NCOLS)

    rows = np.concatenate([
        a["L0_tok_conv_b"], a["L0_tok_out_b"].ravel(), a["L0_tok_ff2_b"].ravel(), a["L0_tok_head_b"],
        a["L0_ffn_bo"], a["L0_ffn_gamma"], a["L0_ffn_beta"], a["L0_txt_ln_gamma"], a["L0_txt_ln_beta"]])
    assert rows.shape == (NROWS,)

    w_bc = np.concatenate([a["L0_attn_W_B"], a["L0_attn_W_C"]], axis=1)
    fold = np.zeros((P, W1), f32)
    fold[np.arange(P), np.arange(P) % W1] = 1.0
    misc = np.concatenate([
        a["L0_tok_head_w"], two_parts(w_bc), two_parts(np.broadcast_to(a["L0_attn_W_D"], (W, P))),
        two_parts(a["L0_ffn_W1"].T), two_parts(a["L0_ffn_W2"]), two_parts(a["L0_ffn_Wo"].T), fold], axis=1)
    assert misc.shape == (P, NMISC)

    shifts = np.zeros((2 * S_TXT, 3, 2 * S_TXT), f32)
    for i in range(3):
        for s in range(2 * S_TXT):
            if 0 <= s % S_TXT + i - 1 < S_TXT:
                shifts[s + i - 1, i, s] = 1.0
    sel = np.zeros((3, 2 * N, NC_, 2, P), f32)
    for c in range(NC_):
        states = [c, c] if c < C0 else [c - C0, c - C0 + C1]
        for half, n in enumerate(states):
            cut = slice(half * W1, (half + 1) * W1)
            sel[:, n, c, 0, cut] = 1.0
            sel[:, N + n, c, 1, cut] = 1.0
    arrays = {
        "ids": a["x_txt"].astype(np.int32).reshape(2 * S_TXT, 1),
        "patches": patches, "convw": convw, "qkvw": qkvw, "outw": outw, "ff1w": ff1w, "ff2w": ff2w,
        "cols": cols, "rows": rows, "misc": misc, "ident": np.eye(P, dtype=f32),
        "tconst": shifts.reshape(2 * S_TXT, NTC),
        "sel": sel.reshape(3 * 2 * N, 2 * NC_, P).astype(ml_dtypes.bfloat16),
        "word_emb": a["L0_txt_word_emb"], "pos_emb": a["L0_txt_pos_emb"],
    }
    nc = bacc.Bacc("TRN2", target_bir_lowering=False, num_devices=1)
    laid, args = {}, []
    for name, arr in arrays.items():
        arr = np.ascontiguousarray(arr)
        laid[f"in_{name}"] = arr
        args.append(nc.dram_tensor(f"in_{name}", arr.shape, mybir.dt.from_np(arr.dtype), kind="ExternalInput").ap())
    args.append(nc.dram_tensor("out", (NB, L, W), F32, kind="ExternalOutput").ap())
    build(nc, *args)
    r = run_bass_kernel_spmd(nc, [laid], core_ids=[0])
    return r.results[0]["out"]
```
